# Optimizing a Trainium2 kernel written in Bass

```python
import numpy as np
import jax
import jax.numpy as jnp

def _softmax(x, axis=-1):
    return jax.nn.softmax(x, axis=axis)

def _gelu(x):
    return jax.nn.gelu(x, approximate=True)

def _silu(x):
    return jax.nn.silu(x)

def _sigmoid(x):
    return jax.nn.sigmoid(x)

def _layernorm(x, axis=-1, eps=1e-05):
    m = jnp.mean(x, axis=axis, keepdims=True)
    v = jnp.var(x, axis=axis, keepdims=True)
    return (x - m) / jnp.sqrt(v + eps)

def _scatter_add(tgt, idx, src, axis=0):
    return tgt.at[idx].add(src)

def _segment_sum(src, seg, n):
    return jax.ops.segment_sum(src, seg, n)
kernel_name = 'mk_xattn_ffn_d1_seqx_r4_8e2e26'

def setup_inputs(seed: int=0):
    np.random.seed(seed)
    _w = jnp.asarray

    def _rec_inputs():
        import jax
        import jax.numpy as jnp
        _rk = jax.random.key(seed)
        x = -0.0003929 + 0.9999 * jax.random.normal(jax.random.fold_in(_rk, 1), (4, 512, 256), jnp.float32)
        _lenS = 512 - jax.random.randint(jax.random.fold_in(_rk, 7), (4,), 0, max(1, 512 // 4) + 1, jnp.int32)
        _lenS2 = 512 - jax.random.randint(jax.random.fold_in(_rk, 8), (4,), 0, max(1, 512 // 4) + 1, jnp.int32)
        _ctx_768P = jax.random.normal(jax.random.fold_in(_rk, 11), (4, 16, 192), jnp.float32)
        _ctx_768c = jax.random.dirichlet(jax.random.fold_in(_rk, 511), 0.3 * jnp.ones((16,), jnp.float32), (4, 512))
        _ctx_768t = jnp.einsum('bsk,bkd->bsd', _ctx_768c, _ctx_768P)
        _ctx_768t = _ctx_768t * jax.lax.rsqrt(jnp.mean(jnp.square(_ctx_768t)) + 1e-12) * 0.953939
        ctx_768 = -7.36909e-05 + 0.999899 * (_ctx_768t + 0.3 * jax.random.normal(jax.random.fold_in(_rk, 611), (4, 512, 192), jnp.float32))
        return (x, ctx_768)
    x, ctx_768 = _rec_inputs()

    def _L0_xattn_setup():
        import jax, jax.numpy as jnp
        import numpy as np
        IMG_DIM, TXT_DIM, HID = (256, 192, 256)
        B, LQ, LK = (8, 512, 512)
        key = jax.random.key(seed)
        ks = jax.random.split(key, 8)
        s_img = 1.0 / np.sqrt(IMG_DIM)
        s_txt = 1.0 / np.sqrt(TXT_DIM)
        return {'image_features': jax.random.normal(ks[0], (B, LQ, IMG_DIM), jnp.float32), 'text_features': jax.random.normal(ks[1], (B, LK, TXT_DIM), jnp.float32), 'Wq': jax.random.uniform(ks[2], (IMG_DIM, HID), jnp.float32, -s_img, s_img), 'bq': jax.random.uniform(ks[3], (HID,), jnp.float32, -s_img, s_img), 'Wk': jax.random.uniform(ks[4], (TXT_DIM, HID), jnp.float32, -s_txt, s_txt), 'bk': jax.random.uniform(ks[5], (HID,), jnp.float32, -s_txt, s_txt), 'Wv': jax.random.uniform(ks[6], (TXT_DIM, HID), jnp.float32, -s_txt, s_txt), 'bv': jax.random.uniform(ks[7], (HID,), jnp.float32, -s_txt, s_txt)}
    _L0_xattn_all = _L0_xattn_setup()
    _L0_xattn_in = {k: v for k, v in _L0_xattn_all.items() if k in ('Wq', 'bq', 'Wk', 'bk', 'Wv', 'bv')}
    del _L0_xattn_all

    def _L0_ffn_setup():
        import jax, jax.numpy as jnp
        import numpy as np
        B, S, H, M, E, K = (4, 512, 256, 1024, 8, 2)
        key = jax.random.key(seed)
        ks = jax.random.split(key, 6)
        x = jax.random.normal(ks[0], (B, S, H), dtype=jnp.float32)
        Wr = jax.random.normal(ks[1], (E, H), dtype=jnp.float32) * (1.0 / np.sqrt(H))
        W1 = jax.random.normal(ks[2], (E, M, H), dtype=jnp.float32) * np.sqrt(2.0 / (H + M))
        b1 = jax.random.normal(ks[3], (E, M), dtype=jnp.float32) * 1e-06
        W2 = jax.random.normal(ks[4], (E, H, M), dtype=jnp.float32) * np.sqrt(2.0 / (H + M))
        b2 = jax.random.normal(ks[5], (E, H), dtype=jnp.float32) * 1e-06
        return {'x': x, 'Wr': Wr, 'W1': W1, 'b1': b1, 'W2': W2, 'b2': b2}
    _L0_ffn_all = _L0_ffn_setup()
    _L0_ffn_in = {k: v for k, v in _L0_ffn_all.items() if k in ('Wr', 'W1', 'b1', 'W2', 'b2')}
    del _L0_ffn_all
    return {'x': x, 'ctx_768': ctx_768, 'L0_xattn_Wq': _L0_xattn_in['Wq'], 'L0_xattn_bq': _L0_xattn_in['bq'], 'L0_xattn_Wk': _L0_xattn_in['Wk'], 'L0_xattn_bk': _L0_xattn_in['bk'], 'L0_xattn_Wv': _L0_xattn_in['Wv'], 'L0_xattn_bv': _L0_xattn_in['bv'], 'L0_ffn_Wr': _L0_ffn_in['Wr'], 'L0_ffn_W1': _L0_ffn_in['W1'], 'L0_ffn_b1': _L0_ffn_in['b1'], 'L0_ffn_W2': _L0_ffn_in['W2'], 'L0_ffn_b2': _L0_ffn_in['b2']}

def reference(x, ctx_768, L0_xattn_Wq, L0_xattn_bq, L0_xattn_Wk, L0_xattn_bk, L0_xattn_Wv, L0_xattn_bv, L0_ffn_Wr, L0_ffn_W1, L0_ffn_b1, L0_ffn_W2, L0_ffn_b2):
    import jax
    import jax.numpy as jnp

    def _L0_xattn_ref(image_features, text_features, Wq, bq, Wk, bk, Wv, bv):
        import jax, jax.numpy as jnp
        import numpy as np
        IMG_DIM, TXT_DIM, HID = (256, 192, 256)
        B, LQ, LK = (8, 512, 512)
        query = jnp.einsum('bqi,ih->bqh', image_features, Wq) + bq
        key = jnp.einsum('bkt,th->bkh', text_features, Wk) + bk
        value = jnp.einsum('bkt,th->bkh', text_features, Wv) + bv
        scale = 1.0 / jnp.sqrt(jnp.asarray(HID, query.dtype))
        scores = jnp.einsum('bqh,bkh->bqk', query, key) * scale
        weights = jax.nn.softmax(scores, axis=-1)
        attended = jnp.einsum('bqk,bkh->bqh', weights, value)
        return attended

    def _L0_ffn_ref(x, Wr, W1, b1, W2, b2):
        import jax, jax.numpy as jnp
        import numpy as np
        B, S, H, M, E, K = (4, 512, 256, 1024, 8, 2)
        logits = jnp.einsum('bsh,eh->bse', x, Wr)
        probs = jax.nn.softmax(logits, axis=-1)
        top_v, top_i = jax.lax.top_k(probs, K)
        top_v = top_v / jnp.sum(top_v, axis=-1, keepdims=True)
        out = jnp.zeros_like(x)
        for e in range(E):
            w_e = jnp.sum(jnp.where(top_i == e, top_v, 0.0), axis=-1)
            h = jnp.einsum('bsh,mh->bsm', x, W1[e]) + b1[e]
            h = jax.nn.gelu(h, approximate=False)
            y = jnp.einsum('bsm,hm->bsh', h, W2[e]) + b2[e]
            out = out + y * w_e[..., None]
        return out
    x = x + _L0_xattn_ref(_layernorm(x, axis=-1), ctx_768, L0_xattn_Wq, L0_xattn_bq, L0_xattn_Wk, L0_xattn_bk, L0_xattn_Wv, L0_xattn_bv)
    x = x + _L0_ffn_ref(_layernorm(x, axis=-1), L0_ffn_Wr, L0_ffn_W1, L0_ffn_b1, L0_ffn_W2, L0_ffn_b2)
    return x

_drawn_inputs = setup_inputs


def setup_inputs(seed=0):
    import zlib

    import numpy as np

    out = dict(_drawn_inputs(seed))
    spreads = {}
    factors = {'L0_xattn_bq': 4.631, 'L0_xattn_bk': 8.0, 'L0_ffn_b1': 8.0, 'L0_ffn_b2': 8.0}
    for name, (base, spread) in spreads.items():
        noise = np.random.default_rng([zlib.crc32(name.encode()), seed]).standard_normal(out[name].shape)
        drawn = base * np.exp(spread * noise) if base else spread * noise
        out[name] = jnp.asarray(drawn.astype(out[name].dtype))
    for name, factor in factors.items():
        out[name] = (out[name] * factor).astype(out[name].dtype)
    return out
```

```python
from contextlib import ExitStack

import concourse.bass as bass
from concourse import mybir

F32 = mybir.dt.float32
ALU = mybir.AluOpType
ACT = mybir.ActivationFunctionType
AX = mybir.AxisListType

P = 128
B, LQ, D = 4, 512, 256
LK, TXT = 512, 192
E, M = 8, 1024
EPS = 1e-5
SCALE = float(D) ** -0.5
QT = LQ // P
KT = LK // P
NT = B * QT
DC = D // P
MC = M // P
TXT2 = TXT - P


def projection_order():
    order = []

    def keys_values(b):
        order.extend([("k", b, 0), ("k", b, 1)] + [("v", b, t) for t in range(KT)])

    def queries(b):
        order.extend([("xt", b, 0), ("xt", b, 1), ("q", b, 0), ("q", b, 1)])

    def route(b):
        order.extend([("x2t", b, 0), ("x2t", b, 1), ("logits", b, 0), ("none", b, 0)])

    for b in range(B):
        keys_values(b)
        if b:
            route(b - 1)
        queries(b)
    route(B - 1)
    return {use: n for n, use in enumerate(order)}


def build(nc, x, ctxT, Wq, bq, Wk, bk, Wv, bv, WrT, W1T, b1, W2T, b2, out):
    uses = projection_order()
    with ExitStack() as ctx:
        def sb(name, shape, dt=F32):
            return ctx.enter_context(nc.sbuf_tensor(name, shape, dt))

        def psum(name, shape, dt=F32):
            return ctx.enter_context(nc.psum_tensor(name, shape, dt))

        def sem(name):
            return ctx.enter_context(nc.semaphore(name))

        ident = sb("ident", [P, P])
        zero = sb("zero", [P, P])
        wq_sb = sb("wq_sb", [P, DC, D])
        wk_sb = sb("wk_sb", [P, 2, D])
        wv_sb = sb("wv_sb", [P, 2, D])
        wr_sb = sb("wr_sb", [P, DC, E])
        bq_sb = sb("bq_sb", [P, DC])
        bqs_sb = sb("bqs_sb", [P, DC])
        bk_sb = sb("bk_sb", [P, DC])
        bv_sb = sb("bv_sb", [P, D])
        half = sb("half", [P, NT])
        rank8 = sb("rank8", [P, QT, E])
        x_sb = sb("x_sb", [P, 2, QT, D])
        ctx_sb = sb("ctx_sb", [P, 2, 2, LK])
        xn = sb("xn", [P, QT, D])
        xnT = sb("xnT", [P, DC, LQ])
        kT = sb("kT", [P, DC, LK])
        qT = sb("qT", [P, DC, LQ])
        v_sb = sb("v_sb", [P, KT, D])
        probs = sb("probs", [P, 2, LK])
        probsT = sb("probsT", [P, 2, KT, P])
        xbv = sb("xbv", [P, QT, D])
        stats = sb("stats", [P, 2, NT, 6])
        mv = sb("mv", [P, 2, NT, 2])
        vare = sb("vare", [P, 2, NT])
        rstd = sb("rstd", [P, 2, NT])
        negmax = sb("negmax", [P, NT])
        rowsum = sb("rowsum", [P, NT])
        rowinv = sb("rowinv", [P, NT])
        acc = sb("acc", [P, NT, D])
        xn2 = sb("xn2", [P, QT, D])
        x2T = sb("x2T", [P, DC, NT * P])
        lg = sb("lg", [P, NT, E])
        ez = sb("ez", [P, NT, E])
        rt = sb("rt", [P, 8, QT, E])
        rc = sb("rc", [P, 12, QT])
        gates = sb("gates", [P, NT, E])
        w1_sb = sb("w1_sb", [P, 2, DC, M])
        w2_sb = sb("w2_sb", [P, 2, MC, D])
        b1_sb = sb("b1_sb", [P, E, MC])
        b2_sb = sb("b2_sb", [P, E, D])
        g_sb = sb("g_sb", [P, MC, LQ])
        yt = sb("yt", [P, 2, D])

        proj = [psum(f"proj{i}", [P, 512]) for i in range(2)]
        s_ps = [psum(f"s_ps{i}", [P, 512]) for i in range(2)]
        t_ps = [psum(f"t_ps{i}", [P, 512]) for i in range(2)]
        o_ps = [psum(f"o_ps{i}", [P, 512]) for i in range(2)]

        w_in = sem("w_in"); b_in = sem("b_in")
        x_in = [sem(f"x_in{i}") for i in range(2)]
        ctx_in = [sem(f"ctx_in{i}") for i in range(2)]
        consts = sem("consts"); bqs_ready = sem("bqs_ready")
        proj_full = sem("proj_full")
        proj_free = [sem("proj_free_act"), sem("proj_free_dve")]
        ln_var = sem("ln_var"); ln_rstd = sem("ln_rstd"); xn_ready = sem("xn_ready")
        ln2_var = sem("ln2_var"); ln2_rstd = sem("ln2_rstd"); xn2_ready = sem("xn2_ready")
        xbv_ready = sem("xbv_ready")
        s_full = sem("s_full"); max_ready = sem("max_ready"); p_ready = sem("p_ready")
        t_full = sem("t_full"); pt_ready = [sem("pt_act"), sem("pt_dve")]
        o_full = sem("o_full"); x2_ready = sem("x2_ready")
        lz_ready = sem("lz_ready"); ez_ready = sem("ez_ready")
        chain = sem("chain"); pchain = sem("pchain")
        w1_in = [sem(f"w1_in{i}") for i in range(2)]
        h_full = sem("h_full"); g_ready = sem("g_ready")
        y_full = sem("y_full"); y_added = sem("y_added")
        stored = sem("stored")

        block = ctx.enter_context(nc.Block())

        @block.sync
        def _(sp):
            for t, a in ((wk_sb, Wk), (wv_sb, Wv)):
                sp.dma_start(t[:, 0, :], a[0:P, :]).then_inc(w_in, 16)
                sp.dma_start(t[0:TXT2, 1, :], a[P:TXT, :]).then_inc(w_in, 16)
            for b in range(B):
                if b >= 2:
                    sp.wait_ge(proj_full, uses["v", b - 2, KT - 1] + 1)
                    sp.wait_ge(xn_ready, b - 1)
                    sp.wait_ge(xbv_ready, b - 1)
                sp.dma_start(ctx_sb[:, b % 2, 0, :], ctxT[b, 0:P, :]).then_inc(ctx_in[b % 2], 16)
                sp.dma_start(ctx_sb[0:TXT2, b % 2, 1, :], ctxT[b, P:TXT, :]).then_inc(ctx_in[b % 2], 16)
                sp.dma_start(x_sb[:, b % 2, :, :], x[b].rearrange("(t p) d -> p t d", p=P)).then_inc(x_in[b % 2], 16)
                if b == 0:
                    sp.dma_start(wq_sb[:], Wq.rearrange("(c p) n -> p c n", p=P)).then_inc(w_in, 16)
                    sp.dma_start(wr_sb[:], WrT.rearrange("(c p) n -> p c n", p=P)).then_inc(w_in, 16)
            for e in range(E):
                if e >= 2:
                    sp.wait_ge(y_full, (e - 1) * NT)
                sp.dma_start(w1_sb[:, e % 2, :, :], W1T[e].rearrange("(c p) m -> p c m", p=P)).then_inc(w1_in[e % 2], 16)
                sp.dma_start(w2_sb[:, e % 2, :, :], W2T[e].rearrange("(c p) d -> p c d", p=P)).then_inc(w1_in[e % 2], 16)
            sp.wait_ge(y_added, E * NT)
            sp.dma_start(out.rearrange("(t p) d -> p t d", p=P), acc[:]).then_inc(stored, 16)
            sp.wait_ge(stored, 16)

        @block.gpsimd
        def _(pool):
            nc.gpsimd.memset(zero[:], 0.0).then_inc(pchain, 1)
            nc.gpsimd.memset(half[:], -0.5).then_inc(consts, 1)
            pool.wait_ge(pchain, 1)
            nc.gpsimd.affine_select(out=ident[:], in_=zero[:], compare_op=ALU.not_equal, fill=1.0, base=0,
                                    pattern=[[-1, P]], channel_multiplier=1).then_inc(consts, 1)
            nc.gpsimd.iota(rank8[:], pattern=[[0, QT], [-1, E]], base=E, channel_multiplier=0,
                           allow_small_or_imprecise_dtypes=True).then_inc(consts, 1)
            pool.dma_start(bq_sb[:], bq).then_inc(b_in, 16)
            pool.dma_start(bk_sb[:], bk).then_inc(b_in, 16)
            pool.dma_start(bv_sb[:], bv.partition_broadcast(P)).then_inc(b_in, 16)
            pool.dma_start(b1_sb[:], b1).then_inc(b_in, 16)
            pool.dma_start(b2_sb[:], b2.partition_broadcast(P)).then_inc(b_in, 16)
            pool.wait_ge(b_in, 80)
            pool.wait_ge(consts, 3)

            def rsqrt(which, b, var, done):
                pool.wait_ge(var, b + 1)
                nc.gpsimd.tensor_tensor(rstd[:, which, b * QT:(b + 1) * QT], vare[:, which, b * QT:(b + 1) * QT],
                                        half[:, b * QT:(b + 1) * QT], ALU.pow).then_inc(done, 1)

            rsqrt(0, 0, ln_var, ln_rstd)
            for b in range(B):
                pool.wait_ge(x_in[b % 2], 16 * (b // 2 + 1))
                if b:
                    pool.wait_ge(x2_ready, QT * b)
                for q in range(QT):
                    i = nc.gpsimd.tensor_tensor(xbv[:, q, :], x_sb[:, b % 2, q, :], bv_sb[:], ALU.add)
                i.then_inc(xbv_ready, 1)
                if b + 1 < B:
                    rsqrt(0, b + 1, ln_var, ln_rstd)
                rsqrt(1, b, ln2_var, ln2_rstd)

        @block.tensor
        def _(pe):
            pe.wait_ge(consts, 3)
            pe.wait_ge(w_in, 96)

            def begin(use):
                n = uses[use]
                if n >= 2:
                    pe.wait_ge(proj_free[n % 2], n // 2)
                return proj[n % 2]

            def keys_values(b):
                pe.wait_ge(ctx_in[b % 2], 32 * (b // 2 + 1))
                rows = [P, TXT2]
                for c in range(DC):
                    bank = begin(("k", b, c))
                    for t in range(2):
                        i = nc.tensor.matmul(bank[:, 0:LK], wk_sb[0:rows[t], t, c * P:(c + 1) * P],
                                             ctx_sb[0:rows[t], b % 2, t, :], start=(t == 0), stop=(t == 1))
                    i.then_inc(proj_full, 1)
                for k in range(KT):
                    bank = begin(("v", b, k))
                    for t in range(2):
                        i = nc.tensor.matmul(bank[:, 0:D], ctx_sb[0:rows[t], b % 2, t, k * P:(k + 1) * P],
                                             wv_sb[0:rows[t], t, :], start=(t == 0), stop=(t == 1))
                    i.then_inc(proj_full, 1)

            def transposed(name, b, src, ready):
                pe.wait_ge(ready, b + 1)
                for c in range(DC):
                    bank = begin((name, b, c))
                    for q in range(QT):
                        i = nc.tensor.transpose(bank[:, q * P:(q + 1) * P], src[:, q, c * P:(c + 1) * P], ident[:])
                    i.then_inc(proj_full, 1)

            def queries(b):
                transposed("xt", b, xn, xn_ready)
                pe.wait_ge(proj_free[0], uses["xt", b, 0] // 2 + 1)
                pe.wait_ge(proj_free[1], uses["xt", b, 1] // 2 + 1)
                for c in range(DC):
                    bank = begin(("q", b, c))
                    for t in range(DC):
                        i = nc.tensor.matmul(bank[:, 0:LQ], wq_sb[:, t, c * P:(c + 1) * P], xnT[:, t, :],
                                             start=(t == 0), stop=(t == DC - 1))
                    i.then_inc(proj_full, 1)

            def scores(b, q):
                n = QT * b + q
                if q == 0:
                    pe.wait_ge(proj_free[0], uses["q", b, 0] // 2 + 1)
                    pe.wait_ge(proj_free[1], uses["q", b, 1] // 2 + 1)
                if n >= 2:
                    pe.wait_ge(p_ready, n - 1)
                for c in range(DC):
                    i = nc.tensor.matmul(s_ps[n % 2][:, 0:LK], qT[:, c, q * P:(q + 1) * P], kT[:, c, :],
                                         start=(c == 0), stop=(c == DC - 1))
                i.then_inc(s_full, 1)

            def turn(b, q):
                n = QT * b + q
                pe.wait_ge(p_ready, n + 1)
                if n >= 2:
                    pe.wait_ge(pt_ready[n % 2], n // 2)
                for k in range(KT):
                    i = nc.tensor.transpose(t_ps[n % 2][:, k * P:(k + 1) * P], probs[:, n % 2, k * P:(k + 1) * P], ident[:])
                i.then_inc(t_full, 1)

            def attend(b, q):
                n = QT * b + q
                pe.wait_ge(pt_ready[n % 2], n // 2 + 1)
                if n >= 2:
                    pe.wait_ge(x2_ready, n - 1)
                for k in range(KT):
                    i = nc.tensor.matmul(o_ps[n % 2][:, 0:D], probsT[:, n % 2, k, :], v_sb[:, k, :],
                                         start=(k == 0), stop=(k == KT - 1))
                i.then_inc(o_full, 1)

            def route(b):
                transposed("x2t", b, xn2, xn2_ready)
                bank = begin(("logits", b, 0))
                pe.wait_ge(proj_free[0], uses["x2t", b, 0] // 2 + 1)
                pe.wait_ge(proj_free[1], uses["x2t", b, 1] // 2 + 1)
                for q in range(QT):
                    for c in range(DC):
                        i = nc.tensor.matmul(bank[:, q * E:(q + 1) * E], x2T[:, c, (QT * b + q) * P:(QT * b + q + 1) * P],
                                             wr_sb[:, c, :], start=(c == 0), stop=(c == DC - 1))
                i.then_inc(proj_full, 2)

            for b in range(B):
                keys_values(b)
                if b:
                    route(b - 1)
                queries(b)
                scores(b, 0)
                scores(b, 1)
                for q in range(QT):
                    turn(b, q)
                    if q + 2 < QT:
                        scores(b, q + 2)
                    attend(b, q)
            route(B - 1)

            for e in range(E):
                pe.wait_ge(w1_in[e % 2], 32 * (e // 2 + 1))
                for b in range(B):
                    for m in range(MC):
                        n = (e * B + b) * MC + m
                        if n >= 2:
                            pe.wait_ge(g_ready, n - 1)
                        else:
                            pe.wait_ge(proj_free[1], uses["x2t", B - 1, 1] // 2 + 2)
                        for c in range(DC):
                            i = nc.tensor.matmul(s_ps[n % 2][:, 0:LQ], w1_sb[:, e % 2, c, m * P:(m + 1) * P],
                                                 x2T[:, c, b * LQ:(b + 1) * LQ], start=(c == 0), stop=(c == DC - 1))
                        i.then_inc(h_full, 1)
                    pe.wait_ge(g_ready, (e * B + b + 1) * MC)
                    for q in range(QT):
                        n = (e * B + b) * QT + q
                        if n >= 2:
                            pe.wait_ge(y_added, n - 1)
                        for m in range(MC):
                            i = nc.tensor.matmul(o_ps[n % 2][:, 0:D], g_sb[:, m, q * P:(q + 1) * P], w2_sb[:, e % 2, m, :],
                                                 start=(m == 0), stop=(m == MC - 1))
                        i.then_inc(y_full, 1)

        @block.scalar
        def _(act):
            act.wait_ge(b_in, 80)
            act.wait_ge(bqs_ready, 1)

            def take(use, out_ap, in_ap, bias=None, scale=1.0):
                n = uses[use]
                act.wait_ge(proj_full, n + 1)
                if bias is None:
                    nc.scalar.activation(out_ap, in_ap, ACT.Copy, scale=scale).then_inc(proj_free[0], 1)
                else:
                    nc.scalar.activation(out_ap, in_ap, ACT.Identity, bias=bias, scale=scale).then_inc(proj_free[0], 1)

            def soft(b, q):
                n = QT * b + q
                act.wait_ge(max_ready, n + 1)
                if n >= 2:
                    act.wait_ge(t_full, n - 1)
                nc.scalar.activation(probs[:, n % 2, :], s_ps[n % 2][:, 0:LK], ACT.Exp, bias=negmax[:, n:n + 1],
                                     accum_out=rowsum[:, n:n + 1]).then_inc(p_ready, 1)

            def take_turned(b, q):
                n = QT * b + q
                act.wait_ge(t_full, n + 1)
                if n >= 2:
                    act.wait_ge(o_full, n - 1)
                nc.scalar.activation(probsT[:, 0, :, :].rearrange("p a b -> p (a b)"), t_ps[0][:], ACT.Copy).then_inc(pt_ready[0], 1)

            def route(b):
                take(("x2t", b, 0), x2T[:, 0, b * LQ:(b + 1) * LQ], proj[0][:])
                take(("logits", b, 0), lg[:, b * QT:(b + 1) * QT, :].rearrange("p a b -> p (a b)"), proj[0][:, 0:QT * E])
                act.wait_ge(lz_ready, b + 1)
                nc.scalar.activation(ez[:, b * QT:(b + 1) * QT, :], rt[:, 0, :, :], ACT.Exp).then_inc(ez_ready, 1)

            for b in range(B):
                take(("k", b, 0), kT[:, 0, :], proj[0][:, 0:LK], bias=bk_sb[:, 0:1])
                take(("v", b, 0), v_sb[:, 0, :], proj[0][:, 0:D])
                take(("v", b, 2), v_sb[:, 2, :], proj[0][:, 0:D])
                if b:
                    route(b - 1)
                take(("xt", b, 0), xnT[:, 0, :], proj[0][:])
                take(("q", b, 0), qT[:, 0, :], proj[0][:], bias=bqs_sb[:, 0:1], scale=SCALE)
                soft(b, 0)
                soft(b, 1)
                take_turned(b, 0)
                soft(b, 2)
                soft(b, 3)
                take_turned(b, 2)
            route(B - 1)
            for e in range(E):
                for b in range(B):
                    if e + b:
                        act.wait_ge(y_full, (e * B + b) * QT)
                    for m in range(MC):
                        n = (e * B + b) * MC + m
                        act.wait_ge(h_full, n + 1)
                        nc.scalar.activation(g_sb[:, m, :], s_ps[n % 2][:, 0:LQ], ACT.Gelu,
                                             bias=b1_sb[:, e, m:m + 1]).then_inc(g_ready, 1)

        @block.vector
        def _(dve):
            steps = [0]

            def link(ins):
                steps[0] += 1
                ins.then_inc(chain, 1)
                dve.wait_ge(chain, steps[0])

            dve.wait_ge(b_in, 80)
            nc.vector.tensor_scalar(bqs_sb[:], bq_sb[:], SCALE, None, ALU.mult).then_inc(bqs_ready, 1)
            dve.wait_ge(consts, 3)

            def take(use, out_ap, in_ap, *ops):
                n = uses[use]
                dve.wait_ge(proj_full, n + 1)
                if ops:
                    nc.vector.tensor_scalar(out_ap, in_ap, *ops).then_inc(proj_free[1], 1)
                else:
                    nc.vector.tensor_copy(out_ap, in_ap).then_inc(proj_free[1], 1)

            def moments(which, n, src):
                link(nc.vector.bn_stats(stats[:, which, n, :], src))
                link(nc.vector.bn_aggr(mv[:, which, n, :], stats[:, which, n, :]))

            def variance(which, b, done):
                s = slice(QT * b, QT * (b + 1))
                nc.vector.tensor_scalar(vare[:, which, s], mv[:, which, s, 1], EPS, None, ALU.add).then_inc(done, 1)

            def normal(which, b, q, dst, src):
                n = QT * b + q
                return nc.vector.tensor_scalar(dst, src, mv[:, which, n, 0:1], rstd[:, which, n:n + 1],
                                               ALU.subtract, ALU.mult)

            def ln1_moments(b):
                dve.wait_ge(x_in[b % 2], 16 * (b // 2 + 1))
                for q in range(QT):
                    moments(0, QT * b + q, x_sb[:, b % 2, q, :])
                variance(0, b, ln_var)

            def ln1_apply(b):
                dve.wait_ge(ln_rstd, b + 1)
                if b:
                    dve.wait_ge(proj_full, uses["xt", b - 1, 1] + 1)
                for q in range(QT):
                    i = normal(0, b, q, xn[:, q, :], x_sb[:, b % 2, q, :])
                i.then_inc(xn_ready, 1)

            def ln2_apply(b):
                dve.wait_ge(ln2_rstd, b + 1)
                if b:
                    dve.wait_ge(proj_full, uses["x2t", b - 1, 1] + 1)
                for q in range(QT):
                    i = normal(1, b, q, xn2[:, q, :], acc[:, QT * b + q, :])
                i.then_inc(xn2_ready, 1)

            def row_max(b, q):
                n = QT * b + q
                dve.wait_ge(s_full, n + 1)
                nc.vector.tensor_reduce(negmax[:, n:n + 1], s_ps[n % 2][:, 0:LK], AX.X, ALU.max,
                                        negate=True).then_inc(max_ready, 1)

            def take_turned(b, q):
                n = QT * b + q
                dve.wait_ge(t_full, n + 1)
                if n >= 2:
                    dve.wait_ge(o_full, n - 1)
                nc.vector.tensor_copy(probsT[:, 1, :, :].rearrange("p a b -> p (a b)"), t_ps[1][:]).then_inc(pt_ready[1], 1)

            def residual(b, q):
                n = QT * b + q
                dve.wait_ge(p_ready, n + 1)
                link(nc.vector.reciprocal(rowinv[:, n:n + 1], rowsum[:, n:n + 1]))
                dve.wait_ge(o_full, n + 1)
                if q == 0:
                    dve.wait_ge(xbv_ready, b + 1)
                nc.vector.scalar_tensor_tensor(out=acc[:, n, :], in0=o_ps[n % 2][:, 0:D], scalar=rowinv[:, n:n + 1],
                                               in1=xbv[:, q, :], op0=ALU.mult, op1=ALU.add).then_inc(x2_ready, 1)
                dve.wait_ge(x2_ready, n + 1)
                moments(1, n, acc[:, n, :])

            def wide(a):
                return a.unsqueeze(2).to_broadcast([P, QT, E])

            def route(b):
                s = slice(QT * b, QT * (b + 1))
                take(("x2t", b, 1), x2T[:, 1, b * LQ:(b + 1) * LQ], proj[1][:])
                dve.wait_ge(proj_free[0], uses["logits", b, 0] // 2 + 1)
                link(nc.vector.tensor_reduce(rc[:, 0, :], lg[:, s, :], AX.X, ALU.max))
                nc.vector.tensor_tensor(rt[:, 0, :, :], lg[:, s, :], wide(rc[:, 0, :]), ALU.subtract).then_inc(lz_ready, 1)
                dve.wait_ge(ez_ready, b + 1)
                link(nc.vector.tensor_reduce(rc[:, 1, :], ez[:, s, :], AX.X, ALU.add))
                link(nc.vector.reciprocal(rc[:, 2, :], rc[:, 1, :]))
                link(nc.vector.tensor_tensor(rt[:, 1, :, :], ez[:, s, :], wide(rc[:, 2, :]), ALU.mult))
                link(nc.vector.tensor_reduce(rc[:, 3, :], rt[:, 1, :, :], AX.X, ALU.max))
                link(nc.vector.tensor_tensor(rt[:, 2, :, :], rt[:, 1, :, :], wide(rc[:, 3, :]), ALU.is_equal))
                link(nc.vector.tensor_tensor(rt[:, 2, :, :], rt[:, 2, :, :], rank8[:], ALU.mult))
                link(nc.vector.tensor_reduce(rc[:, 4, :], rt[:, 2, :, :], AX.X, ALU.max))
                link(nc.vector.tensor_tensor(rt[:, 3, :, :], rank8[:], wide(rc[:, 4, :]), ALU.is_equal))
                link(nc.vector.scalar_tensor_tensor(out=rt[:, 4, :, :], in0=rt[:, 3, :, :], scalar=-2.0,
                                                    in1=rt[:, 1, :, :], op0=ALU.mult, op1=ALU.add))
                link(nc.vector.tensor_reduce(rc[:, 5, :], rt[:, 4, :, :], AX.X, ALU.max))
                link(nc.vector.tensor_tensor(rt[:, 5, :, :], rt[:, 4, :, :], wide(rc[:, 5, :]), ALU.is_equal))
                link(nc.vector.tensor_tensor(rt[:, 5, :, :], rt[:, 5, :, :], rank8[:], ALU.mult))
                link(nc.vector.tensor_reduce(rc[:, 6, :], rt[:, 5, :, :], AX.X, ALU.max))
                link(nc.vector.tensor_tensor(rt[:, 6, :, :], rank8[:], wide(rc[:, 6, :]), ALU.is_equal))
                link(nc.vector.tensor_tensor(rc[:, 7, :], rc[:, 3, :], rc[:, 5, :], ALU.add))
                link(nc.vector.reciprocal(rc[:, 8, :], rc[:, 7, :]))
                link(nc.vector.tensor_tensor(rc[:, 9, :], rc[:, 3, :], rc[:, 8, :], ALU.mult))
                link(nc.vector.tensor_tensor(rc[:, 10, :], rc[:, 5, :], rc[:, 8, :], ALU.mult))
                link(nc.vector.tensor_tensor(rt[:, 3, :, :], rt[:, 3, :, :], wide(rc[:, 9, :]), ALU.mult))
                link(nc.vector.tensor_tensor(rt[:, 6, :, :], rt[:, 6, :, :], wide(rc[:, 10, :]), ALU.mult))
                link(nc.vector.tensor_tensor(gates[:, s, :], rt[:, 3, :, :], rt[:, 6, :, :], ALU.add))
                dve.wait_ge(proj_full, uses["none", b, 0] + 1)
                nc.vector.tensor_copy(rc[:, 11, :], rc[:, 0, :]).then_inc(proj_free[1], 1)

            ln1_moments(0)
            ln1_apply(0)
            for b in range(B):
                take(("k", b, 1), kT[:, 1, :], proj[1][:, 0:LK], bk_sb[:, 1:2], None, ALU.add)
                take(("v", b, 1), v_sb[:, 1, :], proj[1][:, 0:D])
                if b:
                    ln2_apply(b - 1)
                take(("v", b, 3), v_sb[:, 3, :], proj[1][:, 0:D])
                if b:
                    route(b - 1)
                take(("xt", b, 1), xnT[:, 1, :], proj[1][:])
                take(("q", b, 1), qT[:, 1, :], proj[1][:], bq_sb[:, 1:2], SCALE, ALU.add, ALU.mult)
                row_max(b, 0)
                row_max(b, 1)
                row_max(b, 2)
                residual(b, 0)
                take_turned(b, 1)
                row_max(b, 3)
                residual(b, 1)
                residual(b, 2)
                if b + 1 < B:
                    ln1_moments(b + 1)
                take_turned(b, 3)
                residual(b, 3)
                variance(1, b, ln2_var)
                if b + 1 < B:
                    ln1_apply(b + 1)
            ln2_apply(B - 1)
            route(B - 1)

            for e in range(E):
                for b in range(B):
                    for q in range(QT):
                        n = (e * B + b) * QT + q
                        t = QT * b + q
                        dve.wait_ge(y_full, n + 1)
                        link(nc.vector.tensor_tensor(yt[:, n % 2, :], o_ps[n % 2][:, 0:D], b2_sb[:, e, :], ALU.add))
                        nc.vector.scalar_tensor_tensor(out=acc[:, t, :], in0=yt[:, n % 2, :], scalar=gates[:, t, e:e + 1],
                                                       in1=acc[:, t, :], op0=ALU.mult, op1=ALU.add).then_inc(y_added, 1)


def kernel(x, ctx_768, L0_xattn_Wq, L0_xattn_bq, L0_xattn_Wk, L0_xattn_bk, L0_xattn_Wv, L0_xattn_bv,
           L0_ffn_Wr, L0_ffn_W1, L0_ffn_b1, L0_ffn_W2, L0_ffn_b2):
    import numpy as np
    from concourse import bacc
    from concourse.bass_utils import run_bass_kernel_spmd

    def lay(a, *axes):
        a = np.asarray(a)
        return np.ascontiguousarray(a.transpose(*axes) if axes else a)

    arrays = {
        "x": lay(x),
        "ctxT": lay(ctx_768, 0, 2, 1),
        "Wq": lay(L0_xattn_Wq),
        "bq": lay(np.asarray(L0_xattn_bq).reshape(DC, P), 1, 0),
        "Wk": lay(L0_xattn_Wk),
        "bk": lay(np.asarray(L0_xattn_bk).reshape(DC, P), 1, 0),
        "Wv": lay(L0_xattn_Wv),
        "bv": lay(L0_xattn_bv),
        "WrT": lay(L0_ffn_Wr, 1, 0),
        "W1T": lay(L0_ffn_W1, 0, 2, 1),
        "b1": lay(np.asarray(L0_ffn_b1).reshape(E, MC, P), 2, 0, 1),
        "W2T": lay(L0_ffn_W2, 0, 2, 1),
        "b2": lay(L0_ffn_b2),
    }
    nc = bacc.Bacc("TRN2", target_bir_lowering=False, num_devices=1)
    args = [nc.dram_tensor(n, a.shape, mybir.dt.from_np(a.dtype), kind="ExternalInput").ap() for n, a in arrays.items()]
    out = nc.dram_tensor("out", (NT * P, D), F32, kind="ExternalOutput").ap()
    build(nc, *args, out)
    r = run_bass_kernel_spmd(nc, [arrays], core_ids=[0])
    return r.results[0]["out"].reshape(B, LQ, D)
```

```python
from contextlib import ExitStack

import concourse.bass as bass
from concourse import mybir

F32 = mybir.dt.float32
ALU = mybir.AluOpType
ACT = mybir.ActivationFunctionType
AX = mybir.AxisListType

P = 128
B, LQ, D = 4, 512, 256
LK, TXT = 512, 192
E, M = 8, 1024
EPS = 1e-5
SCALE = float(D) ** -0.5
QT = LQ // P
KT = LK // P
NT = B * QT
DC = D // P
MC = M // P
TXT2 = TXT - P
F16 = mybir.dt.float16
BF16 = mybir.dt.bfloat16
I32 = mybir.dt.int32
N = NT * P
ROW = D + 2
REGION = P + N
TILES = 2 * NT + E - 1
UNITS = 2 * E
RING = 2
XR = 4
TAIL = TILES // XR * XR
HALF = MC // 2


def projection_order():
    order = []
    for b in range(B + 1):
        if b < B:
            order += [("k", b, 0), ("k", b, 1)] + [("v", b, t) for t in range(KT)]
        if b:
            order += [("x2t", b - 1, 0), ("x2t", b - 1, 1), ("logits", b - 1, 0)]
        if b < B:
            order += [("xt", b, 0), ("xt", b, 1), ("q", b, 0), ("q", b, 1)]
        if b:
            order += [("rank", b - 1, 0)]
    return {use: n for n, use in enumerate(order)}


def build(nc, x, ctxT, Wq, bq, Wk, bk, Wv, bv, WrT, W1T, b1, W2T, b2, rows, out):
    uses = projection_order()
    with ExitStack() as ctx:
        def psum(name, shape, dt=F32):
            return ctx.enter_context(nc.psum_tensor(name, shape, dt))

        def sem(name):
            return ctx.enter_context(nc.semaphore(name))

        def sb(name, shape, dt=F32, scope=ctx):
            return scope.enter_context(nc.sbuf_tensor(name, shape, dt))

        w1h = sb("w1h", [P, E, DC * M], F16)
        w1l = sb("w1l", [P, E, DC * M], F16)
        w2h = sb("w2h", [P, E, MC * D], F16)
        w2l = sb("w2l", [P, E, MC * D], F16)
        ident = sb("ident", [P, P])
        before = sb("before", [P, P], BF16)
        ones = sb("ones", [P, P], BF16)
        half = sb("half", [P, NT])
        rank8 = sb("rank8", [P, QT, E])
        token = sb("token", [P, NT])
        lane = sb("lane", [P, 1])
        spare = sb("spare", [P, 1])
        b1_sb = sb("b1_sb", [P, E, MC])
        steps128 = sb("steps128", [P, NT])
        tile_no = sb("tile_no", [P, TILES])
        expert_no = sb("expert_no", [P, E])
        none = sb("none", [P, E])
        sq = sb("sq", [P, UNITS, 2])
        total = sb("total", [P, UNITS, 2])
        bound = sb("bound", [P, UNITS, 2])
        power = sb("power", [P, UNITS, 2], I32)
        up = sb("up", [P, UNITS, 2], I32)
        down = sb("down", [P, UNITS, 2], I32)
        undo = sb("undo", [P, E])
        base = sb("base", [P, E])
        nextrow = sb("nextrow", [P, B + 1, E])
        expert_of = sb("expert_of", [P, TILES], I32)
        row_of = sb("row_of", [P, TILES], I32)
        again = sb("again", [P, TILES])

        attn = ExitStack()

        def sa(name, shape, dt=F32):
            return sb(name, shape, dt, attn)

        staged = sa("staged", [P, RING, DC * M])
        wq_sb = sa("wq_sb", [P, DC, D])
        wk_sb = sa("wk_sb", [P, 2, D])
        wv_sb = sa("wv_sb", [P, 2, D])
        wr_sb = sa("wr_sb", [P, DC, E])
        bq_sb = sa("bq_sb", [P, DC])
        bqs_sb = sa("bqs_sb", [P, DC])
        bk_sb = sa("bk_sb", [P, DC])
        bv_sb = sa("bv_sb", [P, D])
        b1q = sa("b1q", [P, E, MC])
        x_sb = sa("x_sb", [P, 2, QT, D])
        ctx_sb = sa("ctx_sb", [P, 2, LK])
        xn = sa("xn", [P, QT, D])
        normT = sa("normT", [P, DC, LQ])
        kT = sa("kT", [P, DC, LK])
        qT = sa("qT", [P, DC, LQ])
        v_sb = sa("v_sb", [P, KT, D])
        probs = sa("probs", [P, 2, LK])
        probsT = sa("probsT", [P, 2, KT, P])
        send = [sa(f"send{k}", [P, QT, ROW]) for k in range(2)]
        stats = sa("stats", [P, 2, NT, 6])
        mv = sa("mv", [P, 2, NT, 2])
        vare = sa("vare", [P, 2, NT])
        rstd = sa("rstd", [P, 2, NT])
        negmax = sa("negmax", [P, NT])
        rowsum = sa("rowsum", [P, NT])
        rowinv = sa("rowinv", [P, NT])
        lg = sa("lg", [P, QT, E])
        ez = sa("ez", [P, QT, E])
        rt = sa("rt", [P, 12, QT, E])
        rc = sa("rc", [P, 12, QT])
        chosen = sa("chosen", [P, QT, E], BF16)
        place = sa("place", [P, B, 2, QT], I32)
        flat_k = kT[:].rearrange("p c n -> p (c n)")
        flat_q = qT[:].rearrange("p c n -> p (c n)")
        tb = flat_q[:, 0:2 * TILES * E].rearrange("p (k t e) -> p k t e", k=2, e=E)
        te = flat_k[:, 0:4 * E].rearrange("p (k e) -> p k e", e=E)
        tv = flat_k[:, 4 * E:4 * E + 7 * TILES].rearrange("p (k t) -> p k t", t=TILES)
        below = flat_k[:, LK:LK + E * NT].rearrange("p (e t) -> p e t", t=NT)
        attn.close()

        moe = ExitStack()

        def sm(name, shape, dt=F32):
            return sb(name, shape, dt, moe)

        b2_sb = sm("b2_sb", [P, E, D])
        xt = sm("xt", [P, XR, ROW])
        xh = sm("xh", [P, 2, DC, P], F16)
        xl = sm("xl", [P, 2, DC, P], F16)
        g = sm("g", [P, 2, MC, P])
        gh = sm("gh", [P, 2, MC, P], F16)
        gl = sm("gl", [P, 2, MC, P], F16)
        y1 = sm("y1", [P, 2, D])
        y2 = sm("y2", [P, 2, D])
        idm = sm("idm", [P, 2, 2])
        idx = sm("idx", [P, 2], I32)
        moe.close()

        proj = [psum(f"proj{i}", [P, 512]) for i in range(2)]
        s_ps = [psum(f"s_ps{i}", [P, 512]) for i in range(2)]
        t_ps = [psum(f"t_ps{i}", [P, 512]) for i in range(2)]
        o_ps = [psum(f"o_ps{i}", [P, 512]) for i in range(2)]
        h_ps = [[s_ps[0], s_ps[1]], [t_ps[0], t_ps[1]]]
        y_ps = o_ps
        xT_ps = proj

        w_in = sem("w_in")
        wr_in = sem("wr_in")
        b_in = sem("b_in")
        x_in = [sem(f"x_in{i}") for i in range(2)]
        ctx_in = sem("ctx_in")
        b2_in = sem("b2_in")
        zeros_set = sem("zeros_set")
        prep = sem("prep")
        consts = sem("consts")
        bqs_ready = sem("bqs_ready")
        b1q_ready = sem("b1q_ready")
        proj_full = sem("proj_full")
        proj_free = [sem("proj_free_act"), sem("proj_free_dve")]
        ln_var = sem("ln_var")
        ln_rstd = sem("ln_rstd")
        xn_ready = sem("xn_ready")
        ln2_var = sem("ln2_var")
        ln2_rstd = sem("ln2_rstd")
        xn2_ready = sem("xn2_ready")
        bv_added = sem("bv_added")
        s_full = sem("s_full")
        max_ready = sem("max_ready")
        p_ready = sem("p_ready")
        t_full = sem("t_full")
        pt_ready = [sem("pt_ready_act"), sem("pt_ready_dve")]
        o_full = sem("o_full")
        x2_ready = sem("x2_ready")
        lz_ready = sem("lz_ready")
        ez_ready = sem("ez_ready")
        chosen_ready = sem("chosen_ready")
        copied = sem("copied")
        gate_ready = sem("gate_ready")
        sent = sem("sent")
        staged_in = [sem(f"staged_in{i}") for i in range(RING)]
        squared = sem("squared")
        summed = sem("summed")
        scale_ready = sem("scale_ready")
        high_ready = sem("high_ready")
        low_ready = sem("low_ready")
        chain = sem("chain")
        tables_ready = sem("tables_ready")
        spare_set = sem("spare_set")
        stored = sem("stored")
        added = sem("added")
        xt_in = [sem(f"xt_in{i}") for i in range(XR)]
        tile_done = sem("tile_done")
        turned = sem("turned")
        xs_ready = sem("xs_ready")
        h_full = sem("h_full")
        g_ready = sem("g_ready")
        gs_ready = sem("gs_ready")
        y_full = sem("y_full")
        y_ready = sem("y_ready")
        xs_high = sem("xs_high")
        g_high = sem("g_high")
        y_biased = sem("y_biased")
        masked = sem("masked")

        def unit_tiles(u):
            e = u // 2
            return (w1h[:, e, :], w1l[:, e, :]) if u % 2 == 0 else (w2h[:, e, :], w2l[:, e, :])

        def wait_rows(eng, t, slot):
            eng.wait_ge(xt_in[slot], t * (16 // XR) + (16 - slot * (16 // XR)))

        block = ctx.enter_context(nc.Block())

        @block.sync
        def _(sp):
            def load_unit(u):
                if u >= RING:
                    sp.wait_ge(low_ready, u - RING + 1)
                src = W1T[u // 2] if u % 2 == 0 else W2T[u // 2]
                c = DC if u % 2 == 0 else MC
                sp.dma_start(staged[:, u % RING, :].rearrange("p (c n) -> p c n", c=c),
                             src.rearrange("(c p) n -> p c n", p=P)).then_inc(staged_in[u % RING], 16)

            def load_ctx(b):
                if b:
                    sp.wait_ge(proj_full, uses["v", b - 1, KT - 1] + 1)
                sp.dma_start(ctx_sb[:, 0, :], ctxT[b, 0:P, :]).then_inc(ctx_in, 16)
                sp.dma_start(ctx_sb[0:TXT2, 1, :], ctxT[b, P:TXT, :]).then_inc(ctx_in, 16)

            def load_x(b):
                if b >= 2:
                    sp.wait_ge(xn2_ready, b - 1)
                    sp.wait_ge(stored, 16 * (b - 1))
                sp.dma_start(x_sb[:, b % 2, :, :], x[b].rearrange("(t p) d -> p t d", p=P)).then_inc(x_in[b % 2], 16)

            load_x(0)
            for t, a in ((wk_sb, Wk), (wv_sb, Wv)):
                sp.dma_start(t[:, 0, :], a[0:P, :]).then_inc(w_in, 16)
                sp.dma_start(t[0:TXT2, 1, :], a[P:TXT, :]).then_inc(w_in, 16)
            load_ctx(0)
            sp.dma_start(wq_sb[:], Wq.rearrange("(c p) n -> p c n", p=P)).then_inc(w_in, 16)
            sp.dma_start(wr_sb[:], WrT.rearrange("(c p) n -> p c n", p=P)).then_inc(wr_in, 16)
            load_x(1)
            for u in range(RING):
                load_unit(u)
            load_ctx(1)
            for b in range(B):
                for q in range(QT):
                    u = RING + QT * b + q
                    if q == 1 and 1 <= b < B - 1:
                        load_ctx(b + 1)
                    if u < UNITS:
                        load_unit(u)
                sp.wait_ge(x2_ready, QT * (b + 1))
                if b:
                    sp.wait_ge(stored, 16 * b)
                sp.dma_start(out[b * LQ:(b + 1) * LQ, :].rearrange("(t p) d -> p t d", p=P),
                             x_sb[:, b % 2, :, :]).then_inc(stored, 16)
                if b + 2 < B:
                    load_x(b + 2)

            sp.wait_ge(tables_ready, 1)
            sp.wait_ge(sent, 32 * NT)
            sp.dma_start(b2_sb[:], b2.partition_broadcast(P)).then_inc(b2_in, 16)

            def load_rows(t, slot):
                if not isinstance(t, int) or t >= XR:
                    sp.wait_ge(tile_done, t - (XR - 1))
                first = sp.value_load(row_of[0:1, bass.ds(t, 1)], min_val=0, max_val=E * REGION - P)
                sp.dma_start(xt[:, slot, :], rows[bass.ds(first, P), :]).then_inc(xt_in[slot], 16)

            for t in range(XR):
                load_rows(t, t)
            with sp.Fori(XR, TAIL - XR + 1, XR) as t:
                for k in range(XR):
                    load_rows(t + k, k)
            for t in range(TAIL, TILES):
                load_rows(t, t % XR)
            sp.wait_ge(stored, 16 * B)
            sp.wait_ge(spare_set, 16)
            sp.wait_ge(added, 16 * TILES)

        @block.gpsimd
        def _(pool):
            pool.dma_start(b1_sb[:], b1).then_inc(b_in, 16)
            pool.dma_start(bq_sb[:], bq).then_inc(b_in, 16)
            pool.dma_start(bk_sb[:], bk).then_inc(b_in, 16)
            pool.dma_start(bv_sb[:], bv.partition_broadcast(P)).then_inc(b_in, 16)
            nc.gpsimd.memset(ident[:], 0.0).then_inc(prep, 1)
            nc.gpsimd.memset(ones[:], 1.0).then_inc(prep, 1)
            nc.gpsimd.memset(send[0][:], 0.0).then_inc(prep, 1)
            nc.gpsimd.memset(half[:], -0.5)
            nc.gpsimd.memset(none[:], 0.0)
            nc.gpsimd.memset(sq[:], 0.0)
            pool.wait_ge(prep, 3)
            nc.gpsimd.affine_select(out=ident[:], in_=ident[:], compare_op=ALU.not_equal, fill=1.0, base=0,
                                    pattern=[[-1, P]], channel_multiplier=1)
            nc.gpsimd.affine_select(out=before[:], in_=ones[:], compare_op=ALU.is_gt, fill=0.0, base=0,
                                    pattern=[[1, P]], channel_multiplier=-1)
            exact = dict(allow_small_or_imprecise_dtypes=True)
            nc.gpsimd.iota(rank8[:], pattern=[[0, QT], [-1, E]], base=E, channel_multiplier=0, **exact)
            nc.gpsimd.iota(token[:], pattern=[[P, NT]], base=0, channel_multiplier=1, **exact)
            nc.gpsimd.iota(steps128[:], pattern=[[P, NT]], base=0, channel_multiplier=0, **exact)
            nc.gpsimd.iota(tile_no[:], pattern=[[1, TILES]], base=0, channel_multiplier=0, **exact)
            nc.gpsimd.iota(expert_no[:], pattern=[[1, E]], base=0, channel_multiplier=0, **exact)
            nc.gpsimd.iota(lane[:], pattern=[[0, 1]], base=0, channel_multiplier=1, **exact)
            nc.gpsimd.iota(spare[:], pattern=[[0, 1]], base=N, channel_multiplier=1, **exact)
            nc.gpsimd.iota(base[:], pattern=[[REGION, E]], base=P, channel_multiplier=0, **exact).then_inc(consts, 1)
            for e in range(E):
                pool.dma_start(rows[e * REGION:e * REGION + P, :], send[0][:, 0, :]).then_inc(zeros_set, 16)
            pool.dma_start(out[N:N + P, :], send[0][:, 1, 0:D]).then_inc(spare_set, 16)
            pool.wait_ge(b_in, 64)

            def rsqrt(which, b, var, done):
                pool.wait_ge(var, b + 1)
                nc.gpsimd.tensor_tensor(rstd[:, which, b * QT:(b + 1) * QT], vare[:, which, b * QT:(b + 1) * QT],
                                        half[:, b * QT:(b + 1) * QT], ALU.pow).then_inc(done, 1)

            def add_all(u):
                pool.wait_ge(squared, u + 1)
                nc.gpsimd.partition_all_reduce(total[:, u, :], sq[:, u, :], P, bass.bass_isa.ReduceOp.add).then_inc(summed, 1)

            def send_rows(b):
                pool.wait_ge(gate_ready, b + 1)
                pool.wait_ge(copied, b + 1)
                for k in range(2):
                    for q in range(QT):
                        pool.indirect_dma_start(out=rows, out_offset=bass.IndirectOffsetOnAxis(ap=place[:, b, k, q:q + 1], axis=0),
                                                in_=send[k][:, q, :], in_offset=None).then_inc(sent, 16)

            pool.wait_ge(b1q_ready, 1)
            rsqrt(0, 0, ln_var, ln_rstd)
            for b in range(B):
                pool.wait_ge(xn_ready, b + 1)
                for q in range(QT):
                    i = nc.gpsimd.tensor_tensor(x_sb[:, b % 2, q, :], x_sb[:, b % 2, q, :], bv_sb[:], ALU.add)
                i.then_inc(bv_added, 1)
                for q in range(QT):
                    u = QT * b + q
                    add_all(u)
                    if q == 2 and b + 1 < B:
                        rsqrt(0, b + 1, ln_var, ln_rstd)
                    if q == 3 and b:
                        send_rows(b - 1)
                rsqrt(1, b, ln2_var, ln2_rstd)
            send_rows(B - 1)

            pool.wait_ge(stored, 16 * B)
            pool.wait_ge(spare_set, 16)

            def scatter(t, u):
                if not isinstance(t, int) or t:
                    pool.wait_ge(added, t * 16)
                pool.wait_ge(y_ready, t + 1)
                pool.sem_inc(tile_done, 1)
                pool.indirect_dma_start(out=out, out_offset=bass.IndirectOffsetOnAxis(ap=idx[:, u:u + 1], axis=0),
                                        in_=y2[:, u, :], in_offset=None, compute_op=ALU.add).then_inc(added, 16)

            scatter(0, 0)
            with pool.Fori(1, TILES - XR - 1, XR) as t:
                for k in range(XR):
                    scatter(t + k, (k + 1) % 2)
            for t in range(TILES - 2, TILES):
                scatter(t, t % 2)

        @block.tensor
        def _(pe):
            pe.wait_ge(consts, 1)
            pe.wait_ge(w_in, 80)
            pe.wait_ge(wr_in, 16)

            def begin(use):
                n = uses[use]
                if n >= 2:
                    pe.wait_ge(proj_free[n % 2], n // 2)
                return proj[n % 2]

            def taken(use):
                pe.wait_ge(proj_free[uses[use] % 2], uses[use] // 2 + 1)

            def keys_values(b):
                pe.wait_ge(ctx_in, 32 * (b + 1))
                part = [P, TXT2]
                for c in range(DC):
                    bank = begin(("k", b, c))
                    for t in range(2):
                        i = nc.tensor.matmul(bank[:, 0:LK], wk_sb[0:part[t], t, c * P:(c + 1) * P],
                                             ctx_sb[0:part[t], t, :], start=(t == 0), stop=(t == 1))
                    i.then_inc(proj_full, 1)
                for k in range(KT):
                    bank = begin(("v", b, k))
                    for t in range(2):
                        i = nc.tensor.matmul(bank[:, 0:D], ctx_sb[0:part[t], t, k * P:(k + 1) * P],
                                             wv_sb[0:part[t], t, :], start=(t == 0), stop=(t == 1))
                    i.then_inc(proj_full, 1)

            def turn_rows(name, b, src):
                for c in range(DC):
                    bank = begin((name, b, c))
                    for q in range(QT):
                        i = nc.tensor.transpose(bank[:, q * P:(q + 1) * P], src[:, q, c * P:(c + 1) * P], ident[:])
                    i.then_inc(proj_full, 1)

            def queries(b):
                pe.wait_ge(xn_ready, b + 1)
                turn_rows("xt", b, xn)
                taken(("xt", b, 0))
                taken(("xt", b, 1))
                for c in range(DC):
                    bank = begin(("q", b, c))
                    for t in range(DC):
                        i = nc.tensor.matmul(bank[:, 0:LQ], wq_sb[:, t, c * P:(c + 1) * P], normT[:, t, :],
                                             start=(t == 0), stop=(t == DC - 1))
                    i.then_inc(proj_full, 1)

            def scores(b, q):
                n = QT * b + q
                if q == 0:
                    taken(("q", b, 0))
                    taken(("q", b, 1))
                if n >= 2:
                    pe.wait_ge(p_ready, n - 1)
                for c in range(DC):
                    i = nc.tensor.matmul(s_ps[n % 2][:, 0:LK], qT[:, c, q * P:(q + 1) * P], kT[:, c, :],
                                         start=(c == 0), stop=(c == DC - 1))
                i.then_inc(s_full, 1)

            def turn_probs(b, q):
                n = QT * b + q
                pe.wait_ge(p_ready, n + 1)
                if n >= 2:
                    pe.wait_ge(pt_ready[n % 2], n // 2)
                for k in range(KT):
                    i = nc.tensor.transpose(t_ps[n % 2][:, k * P:(k + 1) * P], probs[:, n % 2, k * P:(k + 1) * P], ident[:])
                i.then_inc(t_full, 1)

            def attend(b, q):
                n = QT * b + q
                pe.wait_ge(pt_ready[n % 2], n // 2 + 1)
                if n >= 2:
                    pe.wait_ge(x2_ready, n - 1)
                for k in range(KT):
                    i = nc.tensor.matmul(o_ps[n % 2][:, 0:D], probsT[:, n % 2, k, :], v_sb[:, k, :],
                                         start=(k == 0), stop=(k == KT - 1))
                i.then_inc(o_full, 1)

            def logits(b):
                pe.wait_ge(xn2_ready, b + 1)
                turn_rows("x2t", b, send[0])
                bank = begin(("logits", b, 0))
                taken(("x2t", b, 0))
                taken(("x2t", b, 1))
                for q in range(QT):
                    for c in range(DC):
                        i = nc.tensor.matmul(bank[:, q * E:(q + 1) * E], normT[:, c, q * P:(q + 1) * P],
                                             wr_sb[:, c, :], start=(c == 0), stop=(c == DC - 1))
                i.then_inc(proj_full, 1)

            def ranks(b):
                bank = begin(("rank", b, 0))
                pe.wait_ge(chosen_ready, b + 1)
                m = chosen[:].rearrange("p q e -> p (q e)")
                n = QT * E
                nc.tensor.matmul(bank[:, 0:n], before[:], m, start=True, stop=False, skip_group_check=True)
                for k in range(1, QT):
                    nc.tensor.matmul(bank[:, k * E:n], ones[:], m[:, 0:n - k * E], start=False, stop=False,
                                     skip_group_check=True)
                for k in range(QT):
                    i = nc.tensor.matmul(bank[:, n:n + E], ones[:], m[:, k * E:(k + 1) * E], start=False,
                                         stop=(k == QT - 1), skip_group_check=True)
                i.then_inc(proj_full, 1)

            for b in range(B):
                keys_values(b)
                if b:
                    logits(b - 1)
                queries(b)
                scores(b, 0)
                scores(b, 1)
                for q in range(QT):
                    turn_probs(b, q)
                    if q + 2 < QT:
                        scores(b, q + 2)
                    attend(b, q)
                    if b and q == 2:
                        ranks(b - 1)
            logits(B - 1)
            ranks(B - 1)

            pe.wait_ge(tables_ready, 1)
            pe.wait_ge(low_ready, UNITS)

            def turn_tile(t, u, slot):
                wait_rows(pe, t, slot)
                if not isinstance(t, int) or t:
                    pe.wait_ge(xs_ready, t)
                for c in range(DC):
                    i = nc.tensor.transpose(xT_ps[u][:, c * P:(c + 1) * P], xt[:, slot, c * P:(c + 1) * P], ident[:])
                i.then_inc(turned, 1)

            def hidden(t, u):
                e = pe.value_load(expert_of[0:1, bass.ds(t, 1)], min_val=0, max_val=E - 1)
                pe.wait_ge(xs_ready, t + 1)
                if not isinstance(t, int) or t >= 2:
                    pe.wait_ge(g_ready, t * 2 - 2)
                for s in range(2):
                    for m in range(HALF):
                        k = 0
                        for w, r in ((w1h, xh), (w1h, xl), (w1l, xh)):
                            for c in range(DC):
                                at = c * M + (s * HALF + m) * P
                                i = nc.tensor.matmul(h_ps[u][s][:, m * P:(m + 1) * P],
                                                     w[:, bass.ds(e, 1), at:at + P].rearrange("p a n -> p (a n)"),
                                                     r[:, u, c, :], start=(k == 0), stop=(k == 3 * DC - 1))
                                k += 1
                    i.then_inc(h_full, 1)

            def second(t, u):
                e = pe.value_load(expert_of[0:1, bass.ds(t, 1)], min_val=0, max_val=E - 1)
                pe.wait_ge(gs_ready, t * 2 + 2)
                if not isinstance(t, int) or t >= 2:
                    pe.wait_ge(y_ready, t - 1)
                k = 0
                for m in range(MC):
                    for l, w in ((gh, w2h), (gh, w2l), (gl, w2h)):
                        i = nc.tensor.matmul(y_ps[u][:, 0:D], l[:, u, m, :],
                                             w[:, bass.ds(e, 1), m * D:(m + 1) * D].rearrange("p a n -> p (a n)"),
                                             start=(k == 0), stop=(k == 3 * MC - 1))
                        k += 1
                i.then_inc(y_full, 1)

            turn_tile(0, 0, 0)
            hidden(0, 0)
            turn_tile(1, 1, 1)
            hidden(1, 1)
            turn_tile(2, 0, 2)
            second(0, 0)
            with pe.Fori(2, TILES - XR, XR) as t:
                for k in range(4):
                    hidden(t + k, k % 2)
                    turn_tile(t + (k + 1), (k + 1) % 2, (k + 3) % XR)
                    second(t + (k - 1), (k + 1) % 2)
            hidden(TILES - 1, (TILES - 1) % 2)
            second(TILES - 2, (TILES - 2) % 2)
            second(TILES - 1, (TILES - 1) % 2)

        @block.scalar
        def _(act):
            act.wait_ge(bqs_ready, 1)
            act.wait_ge(consts, 1)

            def take(use, out_ap, in_ap, bias=None, scale=1.0):
                n = uses[use]
                if n % 2:
                    return
                act.wait_ge(proj_full, n + 1)
                if bias is None:
                    nc.scalar.activation(out_ap, in_ap, ACT.Copy, scale=scale).then_inc(proj_free[0], 1)
                else:
                    nc.scalar.activation(out_ap, in_ap, ACT.Identity, bias=bias, scale=scale).then_inc(proj_free[0], 1)

            def soft(b, q):
                n = QT * b + q
                act.wait_ge(max_ready, n + 1)
                if n >= 2:
                    act.wait_ge(t_full, n - 1)
                nc.scalar.activation(probs[:, n % 2, :], s_ps[n % 2][:, 0:LK], ACT.Exp, bias=negmax[:, n:n + 1],
                                     accum_out=rowsum[:, n:n + 1]).then_inc(p_ready, 1)

            def take_turned(b, q):
                n = QT * b + q
                act.wait_ge(t_full, n + 1)
                if n >= 2:
                    act.wait_ge(o_full, n - 1)
                nc.scalar.activation(probsT[:, 0, :, :].rearrange("p a b -> p (a b)"), t_ps[0][:], ACT.Copy).then_inc(pt_ready[0], 1)

            def square(u):
                act.wait_ge(staged_in[u % RING], 16 * (u // RING + 1))
                nc.scalar.activation(unit_tiles(u)[1].bitcast(BF16), staged[:, u % RING, :], ACT.Square,
                                     accum_out=sq[:, u, 0:1]).then_inc(squared, 1)

            def high(u):
                act.wait_ge(scale_ready, u + 1)
                nc.scalar.activation(unit_tiles(u)[0], staged[:, u % RING, :], ACT.Copy,
                                     scale=up[:, u, 0:1].bitcast(F32)).then_inc(high_ready, 1)

            def logits(b):
                take(("x2t", b, 0), normT[:, 0, :], proj[0][:])
                take(("x2t", b, 1), normT[:, 1, :], proj[0][:])
                take(("logits", b, 0), lg[:].rearrange("p a b -> p (a b)"), proj[0][:, 0:QT * E])
                if b:
                    act.wait_ge(sent, 32 * QT * b)
                nc.scalar.activation(send[1][:, :, 0:D], send[0][:, :, 0:D], ACT.Copy).then_inc(copied, 1)

            def exps(b):
                act.wait_ge(lz_ready, b + 1)
                nc.scalar.activation(ez[:], rt[:, 0, :, :], ACT.Exp).then_inc(ez_ready, 1)

            for b in range(B):
                take(("k", b, 0), kT[:, 0, :], proj[0][:, 0:LK], bias=bk_sb[:, 0:1])
                take(("k", b, 1), kT[:, 1, :], proj[0][:, 0:LK], bias=bk_sb[:, 1:2])
                for k in range(KT):
                    take(("v", b, k), v_sb[:, k, :], proj[0][:, 0:D])
                if b:
                    logits(b - 1)
                for c in range(DC):
                    take(("xt", b, c), normT[:, c, :], proj[0][:])
                for c in range(DC):
                    take(("q", b, c), qT[:, c, :], proj[0][:], bias=bqs_sb[:, c:c + 1], scale=SCALE)
                for q in range(QT):
                    soft(b, q)
                    if q % 2:
                        take_turned(b, q - 1)
                    if b and q == 1:
                        exps(b - 1)
                    u = QT * b + q
                    square(u)
                    if u:
                        high(u - 1)
            high(UNITS - 1)
            logits(B - 1)
            exps(B - 1)

            act.wait_ge(tables_ready, 1)

            def gelus(t, u):
                e = act.value_load(expert_of[0:1, bass.ds(t, 1)], min_val=0, max_val=E - 1)
                if not isinstance(t, int) or t >= 2:
                    act.wait_ge(gs_ready, t * 2 - 2)
                for s in range(2):
                    act.wait_ge(h_full, t * 2 + (s + 1))
                    for m in range(s * HALF, (s + 1) * HALF):
                        i = nc.scalar.activation(g[:, u, m, :], h_ps[u][s][:, (m % HALF) * P:(m % HALF + 1) * P], ACT.Gelu,
                                                 bias=b1_sb[:, bass.ds(e, 1), m:m + 1].rearrange("p a n -> p (a n)"),
                                                 scale=down[:, bass.ds(e * 2, 1), 0:1].rearrange("p a n -> p (a n)").bitcast(F32))
                    i.then_inc(g_ready, 1)

            gelus(0, 0)
            with act.Fori(1, TILES - 1, 2) as t:
                for k in range(2):
                    gelus(t + k, (k + 1) % 2)

        @block.vector
        def _(dve):
            steps = [0]

            def link(ins):
                steps[0] += 1
                ins.then_inc(chain, 1)
                dve.wait_ge(chain, steps[0])

            dve.wait_ge(b_in, 64)
            dve.wait_ge(consts, 1)
            nc.vector.tensor_scalar(bqs_sb[:], bq_sb[:], SCALE, None, ALU.mult).then_inc(bqs_ready, 1)
            link(nc.vector.tensor_tensor(b1q[:], b1_sb[:], b1_sb[:], ALU.mult))
            link(nc.vector.tensor_scalar(b1q[:], b1q[:], 4.0, None, ALU.mult))
            nc.vector.tensor_reduce(sq[:].rearrange("p (e k) c -> p e k c", k=2)[:, :, 0, 1], b1q[:], AX.X,
                                    ALU.add).then_inc(b1q_ready, 1)
            link(nc.vector.tensor_copy(nextrow[:, 0, :], base[:]))

            def take(use, out_ap, in_ap, *ops):
                n = uses[use]
                if n % 2 == 0:
                    return
                dve.wait_ge(proj_full, n + 1)
                if ops:
                    nc.vector.tensor_scalar(out_ap, in_ap, *ops).then_inc(proj_free[1], 1)
                else:
                    nc.vector.tensor_copy(out_ap, in_ap).then_inc(proj_free[1], 1)

            def moments(which, n, src):
                link(nc.vector.bn_stats(stats[:, which, n, :], src))
                link(nc.vector.bn_aggr(mv[:, which, n, :], stats[:, which, n, :]))

            def variance(which, b, done):
                s = slice(QT * b, QT * (b + 1))
                nc.vector.tensor_scalar(vare[:, which, s], mv[:, which, s, 1], EPS, None, ALU.add).then_inc(done, 1)

            def normal(which, b, q, dst, src):
                n = QT * b + q
                return nc.vector.tensor_scalar(dst, src, mv[:, which, n, 0:1], rstd[:, which, n:n + 1],
                                               ALU.subtract, ALU.mult)

            def ln1_moments(b):
                dve.wait_ge(x_in[b % 2], 16 * (b // 2 + 1))
                for q in range(QT):
                    moments(0, QT * b + q, x_sb[:, b % 2, q, :])
                variance(0, b, ln_var)

            def ln1_apply(b):
                dve.wait_ge(ln_rstd, b + 1)
                if b:
                    dve.wait_ge(proj_full, uses["xt", b - 1, 1] + 1)
                for q in range(QT):
                    i = normal(0, b, q, xn[:, q, :], x_sb[:, b % 2, q, :])
                i.then_inc(xn_ready, 1)

            def ln2_apply(b):
                dve.wait_ge(ln2_rstd, b + 1)
                if b:
                    dve.wait_ge(sent, 32 * QT * b)
                    dve.wait_ge(copied, b)
                else:
                    dve.wait_ge(zeros_set, 16 * E)
                    dve.wait_ge(spare_set, 16)
                for q in range(QT):
                    i = normal(1, b, q, send[0][:, q, 0:D], x_sb[:, b % 2, q, :])
                i.then_inc(xn2_ready, 1)

            def row_max(b, q):
                n = QT * b + q
                dve.wait_ge(s_full, n + 1)
                nc.vector.tensor_reduce(negmax[:, n:n + 1], s_ps[n % 2][:, 0:LK], AX.X, ALU.max,
                                        negate=True).then_inc(max_ready, 1)

            def take_turned(b, q):
                n = QT * b + q
                dve.wait_ge(t_full, n + 1)
                if n >= 2:
                    dve.wait_ge(o_full, n - 1)
                nc.vector.tensor_copy(probsT[:, 1, :, :].rearrange("p a b -> p (a b)"), t_ps[1][:]).then_inc(pt_ready[1], 1)

            def residual(b, q):
                n = QT * b + q
                dve.wait_ge(p_ready, n + 1)
                link(nc.vector.reciprocal(rowinv[:, n:n + 1], rowsum[:, n:n + 1]))
                dve.wait_ge(o_full, n + 1)
                if q == 0:
                    dve.wait_ge(bv_added, b + 1)
                nc.vector.scalar_tensor_tensor(out=x_sb[:, b % 2, q, :], in0=o_ps[n % 2][:, 0:D], scalar=rowinv[:, n:n + 1],
                                               in1=x_sb[:, b % 2, q, :], op0=ALU.mult, op1=ALU.add).then_inc(x2_ready, 1)
                dve.wait_ge(x2_ready, n + 1)
                moments(1, n, x_sb[:, b % 2, q, :])

            def scale(u):
                dve.wait_ge(summed, u + 1)
                link(nc.vector.tensor_scalar(bound[:, u, 0:1], total[:, u, 0:1], 2.0, 2.0 ** -100, ALU.mult, ALU.max))
                link(nc.vector.scalar_tensor_tensor(out=bound[:, u, 1:2], in0=bound[:, u, 0:1], scalar=2.0 * D,
                                                    in1=total[:, u, 1:2], op0=ALU.mult, op1=ALU.add))
                link(nc.vector.tensor_scalar(power[:, u, :], bound[:, u, :].bitcast(I32), 24, None, ALU.logical_shift_right))
                link(nc.vector.tensor_scalar(down[:, u, :], power[:, u, :], 2.0 ** 23, 49 * 2.0 ** 23, ALU.mult, ALU.add))
                nc.vector.tensor_scalar(up[:, u, :], power[:, u, :], -2.0 ** 23, 205 * 2.0 ** 23, ALU.mult,
                                        ALU.add).then_inc(scale_ready, 1)

            def low(u):
                dve.wait_ge(high_ready, u + 1)
                hi, lo = unit_tiles(u)
                nc.vector.scalar_tensor_tensor(out=lo, in0=staged[:, u % RING, :], scalar=up[:, u, 0:1].bitcast(F32),
                                               in1=hi, op0=ALU.mult, op1=ALU.subtract).then_inc(low_ready, 1)

            def wide(a):
                return a.unsqueeze(2).to_broadcast([P, QT, E])

            def route_logits(b):
                dve.wait_ge(proj_free[0], uses["logits", b, 0] // 2 + 1) if uses["logits", b, 0] % 2 == 0 else None
                link(nc.vector.tensor_reduce(rc[:, 0, :], lg[:], AX.X, ALU.max))
                nc.vector.tensor_tensor(rt[:, 0, :, :], lg[:], wide(rc[:, 0, :]), ALU.subtract).then_inc(lz_ready, 1)

            def route_first(b):
                dve.wait_ge(ez_ready, b + 1)
                link(nc.vector.tensor_reduce(rc[:, 1, :], ez[:], AX.X, ALU.add))
                link(nc.vector.reciprocal(rc[:, 2, :], rc[:, 1, :]))
                link(nc.vector.tensor_tensor(rt[:, 1, :, :], ez[:], wide(rc[:, 2, :]), ALU.mult))
                link(nc.vector.tensor_reduce(rc[:, 3, :], rt[:, 1, :, :], AX.X, ALU.max))
                link(nc.vector.tensor_tensor(rt[:, 2, :, :], rt[:, 1, :, :], wide(rc[:, 3, :]), ALU.is_equal))
                link(nc.vector.tensor_tensor(rt[:, 2, :, :], rt[:, 2, :, :], rank8[:], ALU.mult))
                link(nc.vector.tensor_reduce(rc[:, 4, :], rt[:, 2, :, :], AX.X, ALU.max))
                link(nc.vector.tensor_tensor(rt[:, 3, :, :], rank8[:], wide(rc[:, 4, :]), ALU.is_equal))

            def route_second(b):
                link(nc.vector.scalar_tensor_tensor(out=rt[:, 4, :, :], in0=rt[:, 3, :, :], scalar=-2.0,
                                                    in1=rt[:, 1, :, :], op0=ALU.mult, op1=ALU.add))
                link(nc.vector.tensor_reduce(rc[:, 5, :], rt[:, 4, :, :], AX.X, ALU.max))
                link(nc.vector.tensor_tensor(rt[:, 5, :, :], rt[:, 4, :, :], wide(rc[:, 5, :]), ALU.is_equal))
                link(nc.vector.tensor_tensor(rt[:, 5, :, :], rt[:, 5, :, :], rank8[:], ALU.mult))
                link(nc.vector.tensor_reduce(rc[:, 6, :], rt[:, 5, :, :], AX.X, ALU.max))
                link(nc.vector.tensor_tensor(rt[:, 6, :, :], rank8[:], wide(rc[:, 6, :]), ALU.is_equal))
                nc.vector.tensor_tensor(chosen[:], rt[:, 3, :, :], rt[:, 6, :, :], ALU.add).then_inc(chosen_ready, 1)

            def route_gates(b):
                link(nc.vector.tensor_tensor(rc[:, 7, :], rc[:, 3, :], rc[:, 5, :], ALU.add))
                link(nc.vector.reciprocal(rc[:, 8, :], rc[:, 7, :]))
                for k in range(2):
                    nc.vector.tensor_tensor(send[k][:, :, D], rc[:, 3 + 2 * k, :], rc[:, 8, :], ALU.mult)
                    nc.vector.tensor_copy(send[k][:, :, D + 1], token[:, QT * b:QT * (b + 1)])

            def route_places(b):
                bank = proj[1]
                dve.wait_ge(proj_full, uses["rank", b, 0] + 1)
                ahead = nextrow[:, b, :].unsqueeze(1).to_broadcast([P, QT, E])
                link(nc.vector.tensor_tensor(rt[:, 7, :, :], bank[:, 0:QT * E].rearrange("p (q e) -> p q e", e=E), ahead, ALU.add))
                nc.vector.tensor_tensor(nextrow[:, b + 1, :], bank[:, QT * E:QT * E + E], nextrow[:, b, :],
                                        ALU.add).then_inc(proj_free[1], 1)
                for k in range(2):
                    link(nc.vector.tensor_tensor(rt[:, 8 + k, :, :], rt[:, 7, :, :], rt[:, 3 + 3 * k, :, :], ALU.mult))
                    link(nc.vector.tensor_reduce(rc[:, 9 + k, :], rt[:, 8 + k, :, :], AX.X, ALU.add))
                    i = nc.vector.tensor_copy(place[:, b, k, :], rc[:, 9 + k, :])
                i.then_inc(gate_ready, 1)

            def take_logits(b):
                take(("x2t", b, 0), normT[:, 0, :], proj[1][:])
                take(("x2t", b, 1), normT[:, 1, :], proj[1][:])
                take(("logits", b, 0), lg[:].rearrange("p a b -> p (a b)"), proj[1][:, 0:QT * E])

            ln1_moments(0)
            ln1_apply(0)
            for b in range(B):
                take(("k", b, 0), kT[:, 0, :], proj[1][:, 0:LK], bk_sb[:, 0:1], None, ALU.add)
                take(("k", b, 1), kT[:, 1, :], proj[1][:, 0:LK], bk_sb[:, 1:2], None, ALU.add)
                take(("v", b, 0), v_sb[:, 0, :], proj[1][:, 0:D])
                take(("v", b, 1), v_sb[:, 1, :], proj[1][:, 0:D])
                if b:
                    ln2_apply(b - 1)
                take(("v", b, 2), v_sb[:, 2, :], proj[1][:, 0:D])
                take(("v", b, 3), v_sb[:, 3, :], proj[1][:, 0:D])
                if b:
                    take_logits(b - 1)
                for c in range(DC):
                    take(("xt", b, c), normT[:, c, :], proj[1][:])
                for c in range(DC):
                    take(("q", b, c), qT[:, c, :], proj[1][:], bq_sb[:, c:c + 1], SCALE, ALU.add, ALU.mult)
                for q in range(QT):
                    n = QT * b + q
                    row_max(b, q)
                    if b and q == 0:
                        route_logits(b - 1)
                    if q >= 2:
                        residual(b, q - 2)
                    if q % 2 == 0 and q:
                        take_turned(b, q - 1)
                    if b and q == 2:
                        route_first(b - 1)
                        route_second(b - 1)
                    scale(n)
                    if n:
                        low(n - 1)
                    if q == 0 and b + 1 < B:
                        ln1_moments(b + 1)
                    if b and q == 3:
                        route_gates(b - 1)
                        route_places(b - 1)
                residual(b, QT - 2)
                take_turned(b, QT - 1)
                if b + 1 < B:
                    ln1_apply(b + 1)
                residual(b, QT - 1)
                variance(1, b, ln2_var)
            low(UNITS - 1)
            ln2_apply(B - 1)
            take_logits(B - 1)
            route_logits(B - 1)
            route_first(B - 1)
            route_second(B - 1)
            route_gates(B - 1)
            route_places(B - 1)


            for u in range(0, UNITS, 2):
                nc.vector.tensor_tensor(undo[:, u // 2:u // 2 + 1], down[:, u, 1:2].bitcast(F32),
                                        down[:, u + 1, 0:1].bitcast(F32), ALU.mult)
            dve.wait_ge(gate_ready, B)

            def per_tile(a):
                return a.unsqueeze(2).to_broadcast([P, TILES, E])

            def per_expert(a):
                return a.unsqueeze(1).to_broadcast([P, TILES, E])

            count, tiles, last, first = (te[:, k, :] for k in range(4))
            link(nc.vector.tensor_tensor(count, nextrow[:, B, :], base[:], ALU.subtract))
            link(nc.vector.tensor_tensor(below, count.unsqueeze(2).to_broadcast([P, E, NT]),
                                         steps128[:].unsqueeze(1).to_broadcast([P, E, NT]), ALU.is_gt))
            link(nc.vector.tensor_reduce(tiles, below, AX.X, ALU.add))
            link(nc.vector.tensor_tensor_scan(last, tiles, none[:], 0.0, ALU.add, ALU.add))
            link(nc.vector.tensor_tensor(first, last, tiles, ALU.subtract))
            link(nc.vector.tensor_tensor(tb[:, 0], per_tile(tile_no[:]), per_expert(last), ALU.is_ge))
            link(nc.vector.tensor_reduce(tv[:, 0, :], tb[:, 0], AX.X, ALU.add))
            link(nc.vector.tensor_scalar(tv[:, 1, :], tv[:, 0, :], float(E - 1), None, ALU.min))
            nc.vector.tensor_copy(expert_of[:], tv[:, 1, :])
            link(nc.vector.tensor_tensor(tb[:, 1], per_tile(tv[:, 1, :]), per_expert(expert_no[:]), ALU.is_equal))
            link(nc.vector.tensor_tensor(tb[:, 0], tb[:, 1], per_expert(count), ALU.mult))
            link(nc.vector.tensor_reduce(tv[:, 2, :], tb[:, 0], AX.X, ALU.add))
            link(nc.vector.tensor_tensor(tb[:, 0], tb[:, 1], per_expert(first), ALU.mult))
            link(nc.vector.tensor_reduce(tv[:, 3, :], tb[:, 0], AX.X, ALU.add))
            link(nc.vector.tensor_scalar(tv[:, 2, :], tv[:, 2, :], float(P), None, ALU.subtract))
            link(nc.vector.tensor_tensor(tv[:, 4, :], tile_no[:], tv[:, 3, :], ALU.subtract))
            link(nc.vector.tensor_scalar(tv[:, 4, :], tv[:, 4, :], float(P), None, ALU.mult))
            link(nc.vector.tensor_tensor(tv[:, 5, :], tv[:, 4, :], tv[:, 2, :], ALU.min))
            link(nc.vector.tensor_scalar(tv[:, 6, :], tv[:, 1, :], float(REGION), float(P), ALU.mult, ALU.add))
            nc.vector.tensor_tensor(row_of[:], tv[:, 5, :], tv[:, 6, :], ALU.add)
            nc.vector.tensor_tensor(again[:], tv[:, 4, :], tv[:, 5, :], ALU.subtract).then_inc(tables_ready, 1)

            dve.wait_ge(tables_ready, 1)
            dve.wait_ge(b2_in, 16)

            def take_tile(t, u):
                dve.wait_ge(turned, t + 1)
                if not isinstance(t, int) or t >= 2:
                    dve.wait_ge(h_full, t * 2 - 2)
                src = xT_ps[u][:, 0:D].rearrange("p (c n) -> p c n", c=DC)
                nc.vector.tensor_copy(xh[:, u, :, :], src).then_inc(xs_high, 1)
                dve.wait_ge(xs_high, t + 1)
                nc.vector.tensor_tensor(xl[:, u, :, :], src, xh[:, u, :, :], ALU.subtract).then_inc(xs_ready, 1)

            def split(t, u, s, e):
                if s == 0 and (not isinstance(t, int) or t >= 2):
                    dve.wait_ge(y_full, t - 1)
                dve.wait_ge(g_ready, t * 2 + (s + 1))
                m = slice(s * HALF, (s + 1) * HALF)
                by = up[:, bass.ds(e * 2, 1), 1:2].rearrange("p a n -> p (a n)").bitcast(F32)
                nc.vector.tensor_scalar(gh[:, u, m, :], g[:, u, m, :], by, None, ALU.mult).then_inc(g_high, 1)
                dve.wait_ge(g_high, t * 2 + (s + 1))
                nc.vector.scalar_tensor_tensor(out=gl[:, u, m, :], in0=g[:, u, m, :], scalar=by, in1=gh[:, u, m, :],
                                               op0=ALU.mult, op1=ALU.subtract).then_inc(gs_ready, 1)

            def expert(t):
                return dve.value_load(expert_of[0:1, bass.ds(t, 1)], min_val=0, max_val=E - 1)

            def result(t, u, slot):
                e = expert(t)
                if not isinstance(t, int) or t >= 2:
                    dve.wait_ge(added, t * 16 - 16)
                nc.vector.tensor_scalar(idm[:, 0, u:u + 1], lane[:], again[:, bass.ds(t, 1)], None, ALU.is_lt)
                nc.vector.tensor_tensor(idm[:, 1, u:u + 1], spare[:], xt[:, slot, D + 1:D + 2], ALU.subtract).then_inc(masked, 1)
                dve.wait_ge(y_full, t + 1)
                nc.vector.scalar_tensor_tensor(out=y1[:, u, :], in0=y_ps[u][:, 0:D], scalar=undo[:, bass.ds(e, 1)],
                                               in1=b2_sb[:, bass.ds(e, 1), :].rearrange("p a n -> p (a n)"),
                                               op0=ALU.mult, op1=ALU.add).then_inc(y_biased, 1)
                dve.wait_ge(masked, t + 1)
                nc.vector.scalar_tensor_tensor(out=idx[:, u:u + 1], in0=idm[:, 1, u:u + 1], scalar=idm[:, 0, u:u + 1],
                                               in1=xt[:, slot, D + 1:D + 2], op0=ALU.mult, op1=ALU.add)
                dve.wait_ge(y_biased, t + 1)
                nc.vector.tensor_scalar(y2[:, u, :], y1[:, u, :], xt[:, slot, D:D + 1], None, ALU.mult).then_inc(y_ready, 1)

            def both(t, u, nxt):
                e = expert(t)
                split(t, u, 0, e)
                if nxt:
                    take_tile(t + 1, 1 - u)
                split(t, u, 1, e)

            take_tile(0, 0)
            both(0, 0, True)
            both(1, 1, True)
            result(0, 0, 0)
            with dve.Fori(2, TILES - XR, XR) as t:
                for k in range(4):
                    both(t + k, k % 2, True)
                    result(t + (k - 1), (k + 1) % 2, (k + 1) % XR)
            both(TILES - 1, 0, False)
            result(TILES - 2, 1, (TILES - 2) % XR)
            result(TILES - 1, 0, (TILES - 1) % XR)


def kernel(x, ctx_768, L0_xattn_Wq, L0_xattn_bq, L0_xattn_Wk, L0_xattn_bk, L0_xattn_Wv, L0_xattn_bv,
           L0_ffn_Wr, L0_ffn_W1, L0_ffn_b1, L0_ffn_W2, L0_ffn_b2):
    import numpy as np
    from concourse import bacc
    from concourse.bass_utils import run_bass_kernel_spmd

    def lay(a, *axes):
        a = np.asarray(a)
        return np.ascontiguousarray(a.transpose(*axes) if axes else a)

    arrays = {
        "x": lay(x),
        "ctxT": lay(ctx_768, 0, 2, 1),
        "Wq": lay(L0_xattn_Wq),
        "bq": lay(np.asarray(L0_xattn_bq).reshape(DC, P), 1, 0),
        "Wk": lay(L0_xattn_Wk),
        "bk": lay(np.asarray(L0_xattn_bk).reshape(DC, P), 1, 0),
        "Wv": lay(L0_xattn_Wv),
        "bv": lay(L0_xattn_bv),
        "WrT": lay(L0_ffn_Wr, 1, 0),
        "W1T": lay(L0_ffn_W1, 0, 2, 1),
        "b1": lay(np.asarray(L0_ffn_b1).reshape(E, MC, P), 2, 0, 1),
        "W2T": lay(L0_ffn_W2, 0, 2, 1),
        "b2": lay(L0_ffn_b2),
    }
    nc = bacc.Bacc("TRN2", target_bir_lowering=False, num_devices=1)
    args = [nc.dram_tensor(n, a.shape, mybir.dt.from_np(a.dtype), kind="ExternalInput").ap() for n, a in arrays.items()]
    out = nc.dram_tensor("out", (N + P, D), F32, kind="ExternalOutput").ap()
    rows = nc.dram_tensor("rows", (E * REGION, ROW), F32).ap()
    build(nc, *args, rows, out)
    r = run_bass_kernel_spmd(nc, [arrays], core_ids=[0])
    return r.results[0]["out"][:N].reshape(B, LQ, D)
```

```python
from contextlib import ExitStack

import concourse.bass as bass
from concourse import mybir

F32 = mybir.dt.float32
F16 = mybir.dt.float16
BF16 = mybir.dt.bfloat16
I32 = mybir.dt.int32
ALU = mybir.AluOpType
ACT = mybir.ActivationFunctionType
AX = mybir.AxisListType

P = 128
B, LQ, D = 4, 512, 256
LK, TXT = 512, 192
E, M = 8, 1024
EPS = 1e-5
SCALE = float(D) ** -0.5
QT = LQ // P
KT = LK // P
NT = B * QT
DC = D // P
MC = M // P
TXT2 = TXT - P
N = NT * P
ROW = D + 4
TR = 2 * P
REGION = TR + N
TILES = (2 * N + E * (TR - 1)) // TR
UNITS = 2 * E
RING = 3
XR = 2
QUARTERS = 4
MQ = MC // QUARTERS


def projection_order():
    def steps(name, b, count):
        return [(name, b, k) for k in range(count)]

    order = steps("k", 0, DC) + steps("v", 0, KT) + steps("xt", 0, DC) + steps("q", 0, DC)
    for b in range(B):
        if b:
            order += steps("x2t", b - 1, DC) + steps("logits", b - 1, 1)
        if b + 1 < B:
            order += steps("k", b + 1, DC) + steps("xt", b + 1, DC) + steps("v", b + 1, KT) + steps("q", b + 1, DC)
        if b:
            order += steps("rank", b - 1, 1)
    order += steps("x2t", B - 1, DC) + steps("logits", B - 1, 1) + steps("rank", B - 1, 1)
    return {use: n for n, use in enumerate(order)}


def taken_by_vector(use, n):
    return use[0] == "rank" or (use[0] in ("v", "q") and n % 2 == 1)


def build(nc, x, ctxT, Wq, bq, Wk, bk, Wv, bv, WrT, W1T, b1, W2T, b2, rows, out):
    uses = projection_order()
    with ExitStack() as ctx:
        def psum(name, shape, dt=F32):
            return ctx.enter_context(nc.psum_tensor(name, shape, dt))

        def sem(name):
            return ctx.enter_context(nc.semaphore(name))

        def sb(name, shape, dt=F32, scope=ctx):
            return scope.enter_context(nc.sbuf_tensor(name, shape, dt))

        w1h = sb("w1h", [P, E, DC * M], F16)
        w1l = sb("w1l", [P, E, DC * M], F16)
        w2h = sb("w2h", [P, E, MC * D], F16)
        w2l = sb("w2l", [P, E, MC * D], F16)
        ident = sb("ident", [P, P])
        before = sb("before", [P, P], BF16)
        ones = sb("ones", [P, P], BF16)
        half = sb("half", [P, NT])
        rank8 = sb("rank8", [P, QT, E])
        token = sb("token", [P, NT])
        lane = sb("lane", [P, 2])
        spare = sb("spare", [P, 2])
        b1_sb = sb("b1_sb", [P, E, MC])
        steps = sb("steps", [P, N // TR])
        tile_no = sb("tile_no", [P, TILES])
        expert_no = sb("expert_no", [P, E])
        none = sb("none", [P, E])
        sq = sb("sq", [P, UNITS, 2])
        total = sb("total", [P, UNITS, 2])
        bound = sb("bound", [P, UNITS, 2])
        power = sb("power", [P, UNITS, 2], I32)
        up = sb("up", [P, UNITS, 2], I32)
        down = sb("down", [P, UNITS, 2], I32)
        undo = sb("undo", [P, E])
        warm = sb("warm", [P, 2])
        base = sb("base", [P, E])
        nextrow = sb("nextrow", [P, B + 1, E])
        expert_of = sb("expert_of", [P, TILES], I32)
        row_of = sb("row_of", [P, TILES], I32)
        rank_of = sb("rank_of", [P, TILES])
        again = sb("again", [P, TILES])

        attn = ExitStack()

        def sa(name, shape, dt=F32):
            return sb(name, shape, dt, attn)

        staged = sa("staged", [P, RING, DC * M])
        wq_sb = sa("wq_sb", [P, DC, D])
        wk_sb = sa("wk_sb", [P, 2, D])
        wv_sb = sa("wv_sb", [P, 2, D])
        wr_sb = sa("wr_sb", [P, DC, E])
        bq_sb = sa("bq_sb", [P, DC])
        bqs_sb = sa("bqs_sb", [P, DC])
        bk_sb = sa("bk_sb", [P, DC])
        bv_sb = sa("bv_sb", [P, D])
        b1q = sa("b1q", [P, E, MC])
        x_sb = sa("x_sb", [P, 2, QT, D])
        ctx_sb = w2l[:, E - 1, :].bitcast(F32).rearrange("p (c n) -> p c n", c=2)
        xn = w2h[:, E - 1, :].bitcast(F32).rearrange("p (q d) -> p q d", q=QT)
        normT = sa("normT", [P, DC, LQ])
        kT = sa("kT", [P, DC, LK])
        qT = sa("qT", [P, DC, LQ])
        v_sb = sa("v_sb", [P, KT, D])
        probs = sa("probs", [P, 2, LK])
        probsT = sa("probsT", [P, 2, KT, P])
        send = [sa(f"send{k}", [P, QT, ROW]) for k in range(2)]
        stats = sa("stats", [P, 2, NT, 6])
        mv = sa("mv", [P, 2, NT, 2])
        vare = sa("vare", [P, 2, NT])
        rstd = sa("rstd", [P, 2, NT])
        negmax = sa("negmax", [P, NT])
        rowsum = sa("rowsum", [P, NT])
        rowinv = sa("rowinv", [P, NT])
        lg = sa("lg", [P, QT, E])
        ez = sa("ez", [P, QT, E])
        less_top, first_at, first_one, others, second_at, second_one, next_at = (
            sa(name, [P, QT, E]) for name in
            ("less_top", "first_at", "first_one", "others", "second_at", "second_one", "next_at"))
        place_of = sa("place_of", [P, 2, QT, E])
        top, first_exp, second_exp, first8, second8, exp_sum, exp_inv = (
            sa(name, [P, QT]) for name in
            ("top", "first_exp", "second_exp", "first8", "second8", "exp_sum", "exp_inv"))
        place_sum = sa("place_sum", [P, 2, QT])
        chosen = sa("chosen", [P, QT, E], BF16)
        place = sa("place", [P, B, 2, QT], I32)
        flat_k = kT[:].rearrange("p c n -> p (c n)")
        flat_q = qT[:].rearrange("p c n -> p (c n)")
        tile_expert = flat_q[:, 0:2 * TILES * E].rearrange("p (k t e) -> p k t e", k=2, e=E)
        by_expert = flat_k[:, 0:4 * E].rearrange("p (k e) -> p k e", e=E)
        by_tile = flat_k[:, 4 * E:4 * E + 7 * TILES].rearrange("p (k t) -> p k t", t=TILES)
        below = flat_k[:, LK:LK + E * (N // TR)].rearrange("p (e t) -> p e t", t=N // TR)
        attn.close()

        moe = ExitStack()

        def sm(name, shape, dt=F32):
            return sb(name, shape, dt, moe)

        g = sm("g", [P, MC, TR])
        b2_sb = sm("b2_sb", [P, E, D])
        xt = sm("xt", [P, XR, 2, ROW])
        xh = sm("xh", [P, DC, TR], F16)
        xl = sm("xl", [P, DC, TR], F16)
        gh = sm("gh", [P, MC, TR], F16)
        gl = sm("gl", [P, MC, TR], F16)
        y1 = sm("y1", [P, 2, D])
        y2 = sm("y2", [P, 2, 2, D])
        gates = sm("gates", [P, 3, 2])
        moved = sm("moved", [P, 3, 2])
        idx = sm("idx", [P, 2, 2], I32)
        moe.close()

        proj = [psum(f"proj{i}", [P, 512]) for i in range(2)]
        s_ps = [psum(f"s_ps{i}", [P, 512]) for i in range(2)]
        t_ps = [psum(f"t_ps{i}", [P, 512]) for i in range(2)]
        o_ps = [psum(f"o_ps{i}", [P, 512]) for i in range(2)]
        h_ps = [s_ps[0], s_ps[1], t_ps[0], t_ps[1]]
        y_ps = o_ps
        xT_ps = proj[0]

        wk_in = sem("wk_in")
        w_in = sem("w_in")
        wr_in = sem("wr_in")
        bk_in = sem("bk_in")
        b_in = sem("b_in")
        x_in = [sem(f"x_in{i}") for i in range(2)]
        ctx_in = sem("ctx_in")
        b2_in = sem("b2_in")
        zeros_set = sem("zeros_set")
        prep = sem("prep")
        consts = sem("consts")
        bqs_ready = sem("bqs_ready")
        b1q_ready = sem("b1q_ready")
        proj_full = sem("proj_full")
        proj_free = [sem(f"proj_free{i}") for i in range(2)]
        stats1_ready = sem("stats1_ready")
        stats2_ready = sem("stats2_ready")
        ln_var = sem("ln_var")
        ln_rstd = sem("ln_rstd")
        xn_ready = sem("xn_ready")
        ln2_var = sem("ln2_var")
        ln2_rstd = sem("ln2_rstd")
        xn2_ready = sem("xn2_ready")
        bv_added = sem("bv_added")
        s_full = sem("s_full")
        max_ready = sem("max_ready")
        p_ready = sem("p_ready")
        t_full = sem("t_full")
        pt_ready = sem("pt_ready")
        inv_ready = sem("inv_ready")
        o_full = sem("o_full")
        x2_ready = sem("x2_ready")
        lz_ready = sem("lz_ready")
        ez_ready = sem("ez_ready")
        chosen_ready = sem("chosen_ready")
        gate_ready = sem("gate_ready")
        sent = [sem(f"sent{i}") for i in range(2)]
        staged_in = [sem(f"staged_in{i}") for i in range(RING)]
        squared = sem("squared")
        summed = sem("summed")
        scale_ready = sem("scale_ready")
        high_ready = sem("high_ready")
        low_ready = sem("low_ready")
        chain = sem("chain")
        tables_ready = sem("tables_ready")
        spare_set = sem("spare_set")
        stored = sem("stored")
        added = sem("added")
        xt_in = [sem(f"xt_in{i}") for i in range(XR)]
        half_done = sem("half_done")
        turned = sem("turned")
        xs_ready = sem("xs_ready")
        h_full = sem("h_full")
        g_ready = sem("g_ready")
        gs_ready = sem("gs_ready")
        y_full = sem("y_full")
        y_ready = sem("y_ready")
        xs_high = sem("xs_high")
        g_high = sem("g_high")
        y_biased = sem("y_biased")
        marked = sem("marked")
        warmed = sem("warmed")

        def bank_of(*use):
            return proj[uses[use] % 2]

        def unit_tiles(u):
            e = u // 2
            return (w1h[:, e, :], w1l[:, e, :]) if u % 2 == 0 else (w2h[:, e, :], w2l[:, e, :])

        def wait_rows(eng, t, slot):
            eng.wait_ge(xt_in[slot], t * (16 // XR) + (16 - slot * (16 // XR)))

        block = ctx.enter_context(nc.Block())

        @block.sync
        def _(sp):
            def load_unit(u):
                if u >= RING:
                    sp.wait_ge(low_ready, u - RING + 1)
                src = W1T[u // 2] if u % 2 == 0 else W2T[u // 2]
                c = DC if u % 2 == 0 else MC
                sp.dma_start(staged[:, u % RING, :].rearrange("p (c n) -> p c n", c=c),
                             src.rearrange("(c p) n -> p c n", p=P)).then_inc(staged_in[u % RING], 16)

            def load_ctx(b):
                if b:
                    sp.wait_ge(proj_full, uses["v", b - 1, KT - 1] + 1)
                sp.dma_start(ctx_sb[:, 0, :], ctxT[b, 0:P, :]).then_inc(ctx_in, 16)
                sp.dma_start(ctx_sb[0:TXT2, 1, :], ctxT[b, P:TXT, :]).then_inc(ctx_in, 16)

            sp.dma_start(wk_sb[:, 0, :], Wk[0:P, :]).then_inc(wk_in, 16)
            sp.dma_start(wk_sb[0:TXT2, 1, :], Wk[P:TXT, :]).then_inc(wk_in, 16)
            load_ctx(0)
            sp.dma_start(x_sb[:, 0, :, :], x[0].rearrange("(t p) d -> p t d", p=P)).then_inc(x_in[0], 16)
            sp.dma_start(wv_sb[:, 0, :], Wv[0:P, :]).then_inc(w_in, 16)
            sp.dma_start(wv_sb[0:TXT2, 1, :], Wv[P:TXT, :]).then_inc(w_in, 16)
            sp.dma_start(wq_sb[:], Wq.rearrange("(c p) n -> p c n", p=P)).then_inc(w_in, 16)
            sp.dma_start(x_sb[:, 1, :, :], x[1].rearrange("(t p) d -> p t d", p=P)).then_inc(x_in[1], 16)
            sp.dma_start(wr_sb[:], WrT.rearrange("(c p) n -> p c n", p=P)).then_inc(wr_in, 16)
            for u in range(RING):
                load_unit(u)
            load_ctx(1)
            for u in range(RING, UNITS):
                if u % QT == 1 and u // QT + 1 < B:
                    load_ctx(u // QT + 1)
                load_unit(u)

            sp.wait_ge(tables_ready, 1)
            for i in range(2):
                sp.wait_ge(sent[i], 16 * NT)
            sp.wait_ge(stored, 16 * B)
            sp.wait_ge(low_ready, UNITS - 1)

            def load_rows(t, slot):
                if not isinstance(t, int) or t >= XR:
                    sp.wait_ge(half_done, t * 2 - (2 * XR - 2))
                first = sp.value_load(row_of[0:1, bass.ds(t, 1)], min_val=0, max_val=E * REGION - TR)
                sp.dma_start(xt[:, slot, :, :],
                             rows[bass.ds(first, TR), :].rearrange("(h p) d -> p h d", p=P)).then_inc(xt_in[slot], 16)

            load_rows(0, 0)
            load_rows(1, 1)
            sp.dma_start(b2_sb[:], b2.partition_broadcast(P)).then_inc(b2_in, 16)
            load_rows(2, 0)
            with sp.Fori(XR + 1, TILES - 1, XR) as t:
                for k in range(XR):
                    load_rows(t + k, (k + 1) % XR)
            sp.wait_ge(spare_set, 16)
            sp.wait_ge(added, 32 * TILES)

        @block.gpsimd
        def _(pool):
            nc.gpsimd.memset(ident[:], 0.0).then_inc(prep, 1)
            nc.gpsimd.memset(ones[:], 1.0).then_inc(prep, 1)
            nc.gpsimd.memset(send[0][:], 0.0).then_inc(prep, 1)
            nc.gpsimd.memset(half[:], -0.5)
            nc.gpsimd.memset(none[:], 0.0)
            nc.gpsimd.memset(sq[:], 0.0)
            nc.gpsimd.memset(warm[:], 0.0)
            pool.wait_ge(prep, 3)
            nc.gpsimd.affine_select(out=ident[:], in_=ident[:], compare_op=ALU.not_equal, fill=1.0, base=0,
                                    pattern=[[-1, P]], channel_multiplier=1)
            nc.gpsimd.affine_select(out=before[:], in_=ones[:], compare_op=ALU.is_gt, fill=0.0, base=0,
                                    pattern=[[1, P]], channel_multiplier=-1)
            exact = dict(allow_small_or_imprecise_dtypes=True)
            nc.gpsimd.iota(rank8[:], pattern=[[0, QT], [-1, E]], base=E, channel_multiplier=0, **exact)
            nc.gpsimd.iota(token[:], pattern=[[P, NT]], base=0, channel_multiplier=1, **exact)
            nc.gpsimd.iota(steps[:], pattern=[[TR, N // TR]], base=0, channel_multiplier=0, **exact)
            nc.gpsimd.iota(tile_no[:], pattern=[[1, TILES]], base=0, channel_multiplier=0, **exact)
            nc.gpsimd.iota(expert_no[:], pattern=[[1, E]], base=0, channel_multiplier=0, **exact)
            nc.gpsimd.iota(lane[:], pattern=[[P, 2]], base=0, channel_multiplier=1, **exact)
            nc.gpsimd.iota(spare[:], pattern=[[P, 2]], base=N, channel_multiplier=1, **exact)
            nc.gpsimd.iota(base[:], pattern=[[REGION, E]], base=TR, channel_multiplier=0, **exact).then_inc(consts, 1)
            for e in range(E):
                pool.dma_start(rows[e * REGION:e * REGION + TR, :].rearrange("(h p) d -> p h d", p=P),
                               send[0][:, 0:2, :]).then_inc(zeros_set, 16)
            pool.dma_start(out[N:N + TR, :].rearrange("(h p) d -> p h d", p=P),
                           send[0][:, 0:2, 0:D]).then_inc(spare_set, 16)
            pool.wait_ge(b_in, 48)

            def rsqrt(which, b, var, done):
                pool.wait_ge(var, b + 1)
                nc.gpsimd.tensor_tensor(rstd[:, which, b * QT:(b + 1) * QT], vare[:, which, b * QT:(b + 1) * QT],
                                        half[:, b * QT:(b + 1) * QT], ALU.pow).then_inc(done, 1)

            def add_all(u):
                pool.wait_ge(squared, u + 1)
                nc.gpsimd.partition_all_reduce(total[:, u, :], sq[:, u, :], P,
                                               bass.bass_isa.ReduceOp.add).then_inc(summed, 1)

            def add_bv(b):
                pool.wait_ge(xn_ready, b + 1)
                for q in range(QT):
                    nc.gpsimd.tensor_tensor(x_sb[:, b % 2, q, :], x_sb[:, b % 2, q, :], bv_sb[:],
                                            ALU.add).then_inc(bv_added, 1)

            def send_rows(b, k):
                pool.wait_ge(gate_ready, b + 1)
                for q in range(QT):
                    to = bass.IndirectOffsetOnAxis(ap=place[:, b, k, q:q + 1], axis=0)
                    pool.indirect_dma_start(out=rows, out_offset=to, in_=send[b % 2][:, q, :],
                                            in_offset=None).then_inc(sent[b % 2], 16)

            pool.wait_ge(b1q_ready, 1)
            rsqrt(0, 0, ln_var, ln_rstd)
            add_bv(0)
            for b in range(B - 1):
                add_all(QT * b)
                if b >= 2:
                    send_rows(b - 2, 0)
                rsqrt(0, b + 1, ln_var, ln_rstd)
                add_all(QT * b + 1)
                if b >= 2:
                    send_rows(b - 2, 1)
                add_bv(b + 1)
                add_all(QT * b + 2)
                rsqrt(1, b, ln2_var, ln2_rstd)
                add_all(QT * b + 3)
            add_all(UNITS - 4)
            send_rows(B - 3, 0)
            send_rows(B - 3, 1)
            rsqrt(1, B - 1, ln2_var, ln2_rstd)
            add_all(UNITS - 3)
            send_rows(B - 2, 0)
            add_all(UNITS - 2)
            send_rows(B - 2, 1)
            send_rows(B - 1, 0)
            add_all(UNITS - 1)
            send_rows(B - 1, 1)

            pool.wait_ge(stored, 16 * B)
            pool.wait_ge(spare_set, 16)

            def scatter(t, u):
                if not isinstance(t, int) or t:
                    pool.wait_ge(added, t * 32)
                for r in range(2):
                    pool.wait_ge(y_ready, t * 2 + (r + 1))
                    pool.sem_inc(half_done, 1)
                    to = bass.IndirectOffsetOnAxis(ap=idx[:, u, r:r + 1], axis=0)
                    pool.indirect_dma_start(out=out, out_offset=to, in_=y2[:, u, r, :], in_offset=None,
                                            compute_op=ALU.add).then_inc(added, 16)

            scatter(0, 0)
            with pool.Fori(1, TILES - 1, 2) as t:
                for k in range(2):
                    scatter(t + k, (k + 1) % 2)

        @block.tensor
        def _(pe):
            pe.wait_ge(wk_in, 32)

            def begin(use):
                n = uses[use]
                if n >= 2:
                    pe.wait_ge(proj_free[n % 2], n // 2)
                return proj[n % 2]

            def taken(use):
                pe.wait_ge(proj_free[uses[use] % 2], uses[use] // 2 + 1)

            part = [P, TXT2]

            def keys(b):
                pe.wait_ge(ctx_in, 32 * (b + 1))
                for c in range(DC):
                    bank = begin(("k", b, c))
                    for t in range(2):
                        i = nc.tensor.matmul(bank[:, 0:LK], wk_sb[0:part[t], t, c * P:(c + 1) * P],
                                             ctx_sb[0:part[t], t, :], start=(t == 0), stop=(t == 1))
                    i.then_inc(proj_full, 1)

            def values(b):
                for k in range(KT):
                    bank = begin(("v", b, k))
                    for t in range(2):
                        i = nc.tensor.matmul(bank[:, 0:D], ctx_sb[0:part[t], t, k * P:(k + 1) * P],
                                             wv_sb[0:part[t], t, :], start=(t == 0), stop=(t == 1))
                    i.then_inc(proj_full, 1)

            def turn_rows(name, b, src):
                for c in range(DC):
                    bank = begin((name, b, c))
                    for q in range(QT):
                        i = nc.tensor.transpose(bank[:, q * P:(q + 1) * P], src[:, q, c * P:(c + 1) * P], ident[:])
                    i.then_inc(proj_full, 1)

            def turn_x(b):
                pe.wait_ge(xn_ready, b + 1)
                turn_rows("xt", b, xn)

            def queries(b):
                taken(("xt", b, 0))
                taken(("xt", b, 1))
                for c in range(DC):
                    bank = begin(("q", b, c))
                    for t in range(DC):
                        i = nc.tensor.matmul(bank[:, 0:LQ], wq_sb[:, t, c * P:(c + 1) * P], normT[:, t, :],
                                             start=(t == 0), stop=(t == DC - 1))
                    i.then_inc(proj_full, 1)

            def scores(b, q):
                n = QT * b + q
                if q == 0:
                    taken(("q", b, 0))
                    taken(("q", b, 1))
                if n >= 2:
                    pe.wait_ge(p_ready, n - 1)
                for c in range(DC):
                    i = nc.tensor.matmul(s_ps[n % 2][:, 0:LK], qT[:, c, q * P:(q + 1) * P], kT[:, c, :],
                                         start=(c == 0), stop=(c == DC - 1))
                i.then_inc(s_full, 1)

            def turn_probs(b, q):
                n = QT * b + q
                pe.wait_ge(p_ready, n + 1)
                if n >= 2:
                    pe.wait_ge(pt_ready, n - 1)
                for k in range(KT):
                    i = nc.tensor.transpose(t_ps[n % 2][:, k * P:(k + 1) * P], probs[:, n % 2, k * P:(k + 1) * P], ident[:])
                i.then_inc(t_full, 1)

            def attend(b, q):
                n = QT * b + q
                pe.wait_ge(pt_ready, n + 1)
                if n >= 2:
                    pe.wait_ge(x2_ready, n - 1)
                for k in range(KT):
                    i = nc.tensor.matmul(o_ps[n % 2][:, 0:D], probsT[:, n % 2, k, :], v_sb[:, k, :],
                                         start=(k == 0), stop=(k == KT - 1))
                i.then_inc(o_full, 1)

            def turn_normal(b):
                pe.wait_ge(xn2_ready, b + 1)
                turn_rows("x2t", b, send[b % 2])

            def logits(b):
                bank = begin(("logits", b, 0))
                taken(("x2t", b, 0))
                taken(("x2t", b, 1))
                for q in range(QT):
                    for c in range(DC):
                        i = nc.tensor.matmul(bank[:, q * E:(q + 1) * E], normT[:, c, q * P:(q + 1) * P],
                                             wr_sb[:, c, :], start=(c == 0), stop=(c == DC - 1))
                i.then_inc(proj_full, 1)

            def ranks(b):
                bank = begin(("rank", b, 0))
                pe.wait_ge(chosen_ready, b + 1)
                m = chosen[:].rearrange("p q e -> p (q e)")
                n = QT * E
                nc.tensor.matmul(bank[:, 0:n], before[:], m, start=True, stop=False, skip_group_check=True)
                for k in range(1, QT):
                    nc.tensor.matmul(bank[:, k * E:n], ones[:], m[:, 0:n - k * E], start=False, stop=False,
                                     skip_group_check=True)
                for k in range(QT):
                    i = nc.tensor.matmul(bank[:, n:n + E], ones[:], m[:, k * E:(k + 1) * E], start=False,
                                         stop=(k == QT - 1), skip_group_check=True)
                i.then_inc(proj_full, 1)

            keys(0)
            pe.wait_ge(w_in, 48)
            values(0)
            pe.wait_ge(consts, 1)
            turn_x(0)
            queries(0)
            pe.wait_ge(wr_in, 16)
            for b in range(B):
                last = b == B - 1
                scores(b, 0)
                scores(b, 1)
                if b:
                    turn_normal(b - 1)
                turn_probs(b, 0)
                scores(b, 2)
                if b:
                    logits(b - 1)
                turn_probs(b, 1)
                attend(b, 0)
                scores(b, 3)
                turn_probs(b, 2)
                attend(b, 1)
                if not last:
                    keys(b + 1)
                turn_probs(b, 3)
                attend(b, 2)
                if not last:
                    turn_x(b + 1)
                else:
                    ranks(b - 1)
                attend(b, 3)
                if not last:
                    values(b + 1)
                    queries(b + 1)
                    if b:
                        ranks(b - 1)
            turn_normal(B - 1)
            logits(B - 1)
            ranks(B - 1)

            pe.wait_ge(tables_ready, 1)

            def turn_tile(t, slot):
                wait_rows(pe, t, slot)
                for c in range(DC):
                    for r in range(2):
                        i = nc.tensor.transpose(xT_ps[:, c * TR + r * P:c * TR + (r + 1) * P],
                                                xt[:, slot, r, c * P:(c + 1) * P], ident[:])
                i.then_inc(turned, 1)

            def hidden(t, e):
                pe.wait_ge(xs_ready, t + 1)
                for m in range(MC):
                    k = 0
                    for w, r in ((w1h, xh), (w1h, xl), (w1l, xh)):
                        for c in range(DC):
                            at = c * M + m * P
                            i = nc.tensor.matmul(h_ps[m // MQ][:, (m % MQ) * TR:(m % MQ + 1) * TR],
                                                 w[:, bass.ds(e, 1), at:at + P].rearrange("p a n -> p (a n)"),
                                                 r[:, c, :], start=(k == 0), stop=(k == 3 * DC - 1))
                            k += 1
                    if m % MQ == MQ - 1:
                        i.then_inc(h_full, 1)

            def second(t, e):
                for chunks in (range(0, MC - MQ), range(MC - MQ, MC)):
                    for r in range(2):
                        if chunks[0] == 0 and (not isinstance(t, int) or t):
                            pe.wait_ge(y_ready, t * 2 + (r - 1))
                        for m in chunks:
                            if r == 0 and m % MQ == 0:
                                pe.wait_ge(gs_ready, t * QUARTERS + (m // MQ + 1))
                            parts = ((gh, w2h), (gh, w2l), (gl, w2h))
                            for k, (l, w) in enumerate(parts):
                                i = nc.tensor.matmul(y_ps[r][:, 0:D], l[:, m, r * P:(r + 1) * P],
                                                     w[:, bass.ds(e, 1), m * D:(m + 1) * D].rearrange("p a n -> p (a n)"),
                                                     start=(m == 0 and k == 0), stop=(m == MC - 1 and k == 2))
                        if chunks[-1] == MC - 1:
                            i.then_inc(y_full, 1)

            def tile(t, nxt):
                e = pe.value_load(expert_of[0:1, bass.ds(t, 1)], min_val=0, max_val=E - 1)
                hidden(t, e)
                if nxt is not None:
                    turn_tile(t + 1, nxt)
                second(t, e)

            turn_tile(0, 0)
            pe.wait_ge(low_ready, UNITS)
            tile(0, 1)
            tile(1, 0)
            with pe.Fori(2, TILES - 2, 2) as t:
                for k in range(2):
                    tile(t + k, (k + 1) % 2)
            tile(TILES - 1, None)

        @block.scalar
        def _(act):
            act.dma_start(bk_sb[:], bk).then_inc(bk_in, 16)
            act.dma_start(bq_sb[:], bq).then_inc(b_in, 16)
            act.dma_start(b1_sb[:], b1).then_inc(b_in, 16)
            act.dma_start(bv_sb[:], bv.partition_broadcast(P)).then_inc(b_in, 16)
            act.wait_ge(bk_in, 16)

            def take(use, out_ap, in_ap, bias=None, scale=1.0):
                n = uses[use]
                if taken_by_vector(use, n):
                    return
                act.wait_ge(proj_full, n + 1)
                if bias is None:
                    nc.scalar.activation(out_ap, in_ap, ACT.Copy, scale=scale).then_inc(proj_free[n % 2], 1)
                else:
                    nc.scalar.activation(out_ap, in_ap, ACT.Identity, bias=bias, scale=scale).then_inc(proj_free[n % 2], 1)

            def soft(b, q):
                n = QT * b + q
                act.wait_ge(max_ready, n + 1)
                if n >= 2:
                    act.wait_ge(t_full, n - 1)
                nc.scalar.activation(probs[:, n % 2, :], s_ps[n % 2][:, 0:LK], ACT.Exp, bias=negmax[:, n:n + 1],
                                     accum_out=rowsum[:, n:n + 1]).then_inc(p_ready, 1)

            def take_turned(b, q):
                n = QT * b + q
                act.wait_ge(t_full, n + 1)
                if n >= 2:
                    act.wait_ge(o_full, n - 1)
                nc.scalar.activation(probsT[:, n % 2, :, :].rearrange("p a b -> p (a b)"), t_ps[n % 2][:],
                                     ACT.Copy).then_inc(pt_ready, 1)

            def square(u):
                act.wait_ge(staged_in[u % RING], 16 * (u // RING + 1))
                nc.scalar.activation(unit_tiles(u)[1].bitcast(BF16), staged[:, u % RING, :], ACT.Square,
                                     accum_out=sq[:, u, 0:1]).then_inc(squared, 1)

            def high(u):
                act.wait_ge(scale_ready, u + 1)
                nc.scalar.activation(unit_tiles(u)[0], staged[:, u % RING, :], ACT.Copy,
                                     scale=up[:, u, 0:1].bitcast(F32)).then_inc(high_ready, 1)

            def exps(b):
                act.wait_ge(lz_ready, b + 1)
                nc.scalar.activation(ez[:], less_top[:], ACT.Exp).then_inc(ez_ready, 1)

            def keys(b):
                for c in range(DC):
                    take(("k", b, c), kT[:, c, :], bank_of("k", b, c)[:, 0:LK], bias=bk_sb[:, c:c + 1])

            def values(b):
                for k in range(KT):
                    take(("v", b, k), v_sb[:, k, :], bank_of("v", b, k)[:, 0:D])

            def queries(b):
                for c in range(DC):
                    take(("q", b, c), qT[:, c, :], bank_of("q", b, c)[:, 0:LQ], bias=bqs_sb[:, c:c + 1], scale=SCALE)

            def turned_rows(name, b):
                for c in range(DC):
                    take((name, b, c), normT[:, c, :], bank_of(name, b, c)[:])

            def take_logits(b):
                take(("logits", b, 0), lg[:].rearrange("p a b -> p (a b)"), bank_of("logits", b, 0)[:, 0:QT * E])

            def store(b):
                act.wait_ge(x2_ready, QT * (b + 1))
                if b:
                    act.wait_ge(stored, 16 * b)
                act.dma_start(out[b * LQ:(b + 1) * LQ, :].rearrange("(t p) d -> p t d", p=P),
                              x_sb[:, b % 2, :, :]).then_inc(stored, 16)

            def load_x(b):
                act.wait_ge(xn2_ready, b - 1)
                act.wait_ge(stored, 16 * (b - 1))
                act.dma_start(x_sb[:, b % 2, :, :], x[b].rearrange("(t p) d -> p t d", p=P)).then_inc(x_in[b % 2], 16)

            keys(0)
            values(0)
            turned_rows("xt", 0)
            act.wait_ge(bqs_ready, 1)
            queries(0)
            act.wait_ge(consts, 1)

            for b in range(B):
                u = QT * b
                soft(b, 0)
                if b:
                    store(b - 1)
                soft(b, 1)
                if b:
                    turned_rows("x2t", b - 1)
                take_turned(b, 0)
                if b:
                    high(u - 1)
                square(u)
                if b and b + 1 < B:
                    load_x(b + 1)
                soft(b, 2)
                if b:
                    take_logits(b - 1)
                take_turned(b, 1)
                if b:
                    exps(b - 1)
                soft(b, 3)
                take_turned(b, 2)
                if b + 1 < B:
                    high(u)
                    square(u + 1)
                    keys(b + 1)
                    take_turned(b, 3)
                    high(u + 1)
                    turned_rows("xt", b + 1)
                    square(u + 2)
                    values(b + 1)
                    high(u + 2)
                    queries(b + 1)
                    square(u + 3)
                else:
                    take_turned(b, 3)
            high(UNITS - 4)
            square(UNITS - 3)
            store(B - 1)
            high(UNITS - 3)
            turned_rows("x2t", B - 1)
            square(UNITS - 2)
            take_logits(B - 1)
            exps(B - 1)
            high(UNITS - 2)
            square(UNITS - 1)
            high(UNITS - 1)

            def gelu_table():
                nc.scalar.activation(warm[:, 1:2], warm[:, 0:1], ACT.Gelu).then_inc(warmed, 1)

            gelu_table()
            act.wait_ge(warmed, 1)
            act.wait_ge(tables_ready, 1)

            def gelus(t):
                e = act.value_load(expert_of[0:1, bass.ds(t, 1)], min_val=0, max_val=E - 1)
                by = down[:, bass.ds(e * 2, 1), 0:1].rearrange("p a n -> p (a n)").bitcast(F32)
                for s in range(QUARTERS):
                    act.wait_ge(h_full, t * QUARTERS + (s + 1))
                    for m in range(s * MQ, (s + 1) * MQ):
                        i = nc.scalar.activation(g[:, m, :], h_ps[s][:, (m % MQ) * TR:(m % MQ + 1) * TR], ACT.Gelu,
                                                 bias=b1_sb[:, bass.ds(e, 1), m:m + 1].rearrange("p a n -> p (a n)"),
                                                 scale=by)
                    i.then_inc(g_ready, 1)

            gelus(0)
            with act.Fori(1, TILES - 1, 2) as t:
                gelu_table()
                gelus(t)
                act.wait_ge(warmed, (t + 3) // 2)
                gelus(t + 1)

        @block.vector
        def _(dve):
            links = [0]

            def link(ins):
                links[0] += 1
                ins.then_inc(chain, 1)
                dve.wait_ge(chain, links[0])

            def set_out():
                dve.wait_ge(b_in, 48)
                dve.wait_ge(consts, 1)
                nc.vector.tensor_scalar(bqs_sb[:], bq_sb[:], SCALE, None, ALU.mult).then_inc(bqs_ready, 1)
                link(nc.vector.tensor_tensor(b1q[:], b1_sb[:], b1_sb[:], ALU.mult))
                link(nc.vector.tensor_scalar(b1q[:], b1q[:], 4.0, None, ALU.mult))
                nc.vector.tensor_reduce(sq[:].rearrange("p (e k) c -> p e k c", k=2)[:, :, 0, 1], b1q[:], AX.X,
                                        ALU.add).then_inc(b1q_ready, 1)
                link(nc.vector.tensor_copy(nextrow[:, 0, :], base[:]))

            def take(use, out_ap, in_ap, *ops):
                n = uses[use]
                if not taken_by_vector(use, n):
                    return
                dve.wait_ge(proj_full, n + 1)
                if ops:
                    nc.vector.tensor_scalar(out_ap, in_ap, *ops).then_inc(proj_free[n % 2], 1)
                else:
                    nc.vector.tensor_copy(out_ap, in_ap).then_inc(proj_free[n % 2], 1)

            def aggregate(which, b, ready, done):
                dve.wait_ge(ready, QT * (b + 1))
                for q in range(QT):
                    i = nc.vector.bn_aggr(mv[:, which, QT * b + q, :], stats[:, which, QT * b + q, :])
                link(i)
                tiles = slice(QT * b, QT * (b + 1))
                nc.vector.tensor_scalar(vare[:, which, tiles], mv[:, which, tiles, 1], EPS, None, ALU.add).then_inc(done, 1)

            def normal(which, b, q, dst, src):
                n = QT * b + q
                return nc.vector.tensor_scalar(dst, src, mv[:, which, n, 0:1], rstd[:, which, n:n + 1],
                                               ALU.subtract, ALU.mult)

            def ln1_moments(b):
                dve.wait_ge(x_in[b % 2], 16 * (b // 2 + 1))
                for q in range(QT):
                    nc.vector.bn_stats(stats[:, 0, QT * b + q, :], x_sb[:, b % 2, q, :]).then_inc(stats1_ready, 1)
                aggregate(0, b, stats1_ready, ln_var)

            def ln1_apply(b):
                dve.wait_ge(ln_rstd, b + 1)
                if b:
                    dve.wait_ge(proj_full, uses["xt", b - 1, 1] + 1)
                for q in range(QT):
                    i = normal(0, b, q, xn[:, q, :], x_sb[:, b % 2, q, :])
                i.then_inc(xn_ready, 1)

            def ln2_apply(b):
                dve.wait_ge(ln2_rstd, b + 1)
                if b >= 2:
                    dve.wait_ge(sent[b % 2], 32 * QT * (b // 2))
                if b == 0:
                    dve.wait_ge(zeros_set, 16 * E)
                    dve.wait_ge(spare_set, 16)
                for q in range(QT):
                    i = normal(1, b, q, send[b % 2][:, q, 0:D], x_sb[:, b % 2, q, :])
                i.then_inc(xn2_ready, 1)

            def row_max(b, q):
                n = QT * b + q
                dve.wait_ge(s_full, n + 1)
                nc.vector.tensor_reduce(negmax[:, n:n + 1], s_ps[n % 2][:, 0:LK], AX.X, ALU.max,
                                        negate=True).then_inc(max_ready, 1)

            def invert(b, q):
                n = QT * b + q
                dve.wait_ge(p_ready, n + 1)
                nc.vector.reciprocal(rowinv[:, n:n + 1], rowsum[:, n:n + 1]).then_inc(inv_ready, 1)

            def residual(b, q):
                n = QT * b + q
                dve.wait_ge(inv_ready, n + 1)
                dve.wait_ge(o_full, n + 1)
                dve.wait_ge(bv_added, n + 1)
                nc.vector.scalar_tensor_tensor(out=x_sb[:, b % 2, q, :], in0=o_ps[n % 2][:, 0:D], scalar=rowinv[:, n:n + 1],
                                               in1=x_sb[:, b % 2, q, :], op0=ALU.mult, op1=ALU.add).then_inc(x2_ready, 1)
                dve.wait_ge(x2_ready, n + 1)
                nc.vector.bn_stats(stats[:, 1, n, :], x_sb[:, b % 2, q, :]).then_inc(stats2_ready, 1)

            def scale(u):
                dve.wait_ge(summed, u + 1)
                nc.vector.tensor_scalar(bound[:, u, 0:1], total[:, u, 0:1], 2.0, 2.0 ** -100, ALU.mult, ALU.max)
                link(nc.vector.scalar_tensor_tensor(out=bound[:, u, 1:2], in0=total[:, u, 0:1], scalar=4.0 * D,
                                                    in1=total[:, u, 1:2], op0=ALU.mult, op1=ALU.add))
                link(nc.vector.tensor_scalar(power[:, u, :], bound[:, u, :].bitcast(I32), 24, None,
                                             ALU.logical_shift_right))
                link(nc.vector.tensor_scalar(down[:, u, :], power[:, u, :], 2.0 ** 23, 49 * 2.0 ** 23, ALU.mult, ALU.add))
                nc.vector.tensor_scalar(up[:, u, :], power[:, u, :], -2.0 ** 23, 205 * 2.0 ** 23, ALU.mult,
                                        ALU.add).then_inc(scale_ready, 1)

            def low(u):
                dve.wait_ge(high_ready, u + 1)
                hi, lo = unit_tiles(u)
                nc.vector.scalar_tensor_tensor(out=lo, in0=staged[:, u % RING, :], scalar=up[:, u, 0:1].bitcast(F32),
                                               in1=hi, op0=ALU.mult, op1=ALU.subtract).then_inc(low_ready, 1)

            def wide(a):
                return a.unsqueeze(2).to_broadcast([P, QT, E])

            def route_logits(b):
                n = uses["logits", b, 0]
                dve.wait_ge(proj_free[n % 2], n // 2 + 1)
                link(nc.vector.tensor_reduce(top[:], lg[:], AX.X, ALU.max))
                nc.vector.tensor_tensor(less_top[:], lg[:], wide(top[:]), ALU.subtract).then_inc(lz_ready, 1)

            def route_first(b):
                dve.wait_ge(lz_ready, b + 1)
                link(nc.vector.scalar_tensor_tensor(out=first_at[:], in0=less_top[:], scalar=0.0, in1=rank8[:],
                                                    op0=ALU.is_equal, op1=ALU.mult))
                link(nc.vector.tensor_reduce(first8[:], first_at[:], AX.X, ALU.max))
                link(nc.vector.tensor_tensor(first_one[:], rank8[:], wide(first8[:]), ALU.is_equal))

            def route_second(b):
                dve.wait_ge(ez_ready, b + 1)
                nc.vector.tensor_reduce(first_exp[:], ez[:], AX.X, ALU.max)
                link(nc.vector.scalar_tensor_tensor(out=others[:], in0=first_one[:], scalar=-2.0,
                                                    in1=ez[:], op0=ALU.mult, op1=ALU.add))
                link(nc.vector.tensor_reduce(second_exp[:], others[:], AX.X, ALU.max))
                link(nc.vector.tensor_tensor(second_at[:], others[:], wide(second_exp[:]), ALU.is_equal))
                link(nc.vector.tensor_tensor(second_at[:], second_at[:], rank8[:], ALU.mult))
                link(nc.vector.tensor_reduce(second8[:], second_at[:], AX.X, ALU.max))
                link(nc.vector.tensor_tensor(second_one[:], rank8[:], wide(second8[:]), ALU.is_equal))
                nc.vector.tensor_tensor(chosen[:], first_one[:], second_one[:], ALU.add).then_inc(chosen_ready, 1)

            def route_gates(b):
                to = send[b % 2]
                link(nc.vector.tensor_tensor(exp_sum[:], first_exp[:], second_exp[:], ALU.add))
                link(nc.vector.reciprocal(exp_inv[:], exp_sum[:]))
                nc.vector.tensor_tensor(to[:, :, D], first_exp[:], exp_inv[:], ALU.mult)
                nc.vector.tensor_tensor(to[:, :, D + 1], second_exp[:], exp_inv[:], ALU.mult)
                nc.vector.tensor_copy(to[:, :, D + 2], first8[:])
                nc.vector.tensor_copy(to[:, :, D + 3], token[:, QT * b:QT * (b + 1)])

            def route_places(b):
                n = uses["rank", b, 0]
                bank = proj[n % 2]
                dve.wait_ge(proj_full, n + 1)
                ahead = nextrow[:, b, :].unsqueeze(1).to_broadcast([P, QT, E])
                rank = bank[:, 0:QT * E].rearrange("p (q e) -> p q e", e=E)
                link(nc.vector.tensor_tensor(next_at[:], rank, ahead, ALU.add))
                nc.vector.tensor_tensor(nextrow[:, b + 1, :], bank[:, QT * E:QT * E + E], nextrow[:, b, :],
                                        ALU.add).then_inc(proj_free[n % 2], 1)
                nc.vector.tensor_tensor(place_of[:, 0], next_at[:], first_one[:], ALU.mult)
                link(nc.vector.tensor_tensor(place_of[:, 1], next_at[:], second_one[:], ALU.mult))
                link(nc.vector.tensor_reduce(place_sum[:], place_of[:], AX.X, ALU.add))
                nc.vector.tensor_copy(place[:, b, :, :], place_sum[:]).then_inc(gate_ready, 1)

            def keys(b):
                for c in range(DC):
                    take(("k", b, c), kT[:, c, :], bank_of("k", b, c)[:, 0:LK], bk_sb[:, c:c + 1], None, ALU.add)

            def values(b, chunks=range(KT)):
                for k in chunks:
                    take(("v", b, k), v_sb[:, k, :], bank_of("v", b, k)[:, 0:D])

            def queries(b):
                for c in range(DC):
                    take(("q", b, c), qT[:, c, :], bank_of("q", b, c)[:, 0:LQ], bq_sb[:, c:c + 1], SCALE, ALU.add, ALU.mult)

            ln1_moments(0)
            set_out()
            dve.wait_ge(bk_in, 16)
            keys(0)
            ln1_apply(0)
            values(0)
            queries(0)
            for b in range(B):
                u = QT * b
                row_max(b, 0)
                if b >= 2:
                    route_places(b - 2)
                row_max(b, 1)
                if b:
                    low(u - 2)
                row_max(b, 2)
                invert(b, 0)
                scale(u)
                if b:
                    low(u - 1)
                    route_logits(b - 1)
                residual(b, 0)
                row_max(b, 3)
                invert(b, 1)
                if b + 1 < B:
                    ln1_moments(b + 1)
                    keys(b + 1)
                    ln1_apply(b + 1)
                    residual(b, 1)
                    if b:
                        route_first(b - 1)
                    scale(u + 1)
                    invert(b, 2)
                    invert(b, 3)
                    low(u)
                    residual(b, 2)
                    residual(b, 3)
                    values(b + 1, (0, 1))
                    aggregate(1, b, stats2_ready, ln2_var)
                    values(b + 1, (2, 3))
                    scale(u + 2)
                    if b:
                        route_second(b - 1)
                        route_gates(b - 1)
                    ln2_apply(b)
                    queries(b + 1)
                    low(u + 1)
                    scale(u + 3)
            residual(B - 1, 1)
            route_first(B - 2)
            route_second(B - 2)
            invert(B - 1, 2)
            invert(B - 1, 3)
            route_gates(B - 2)
            residual(B - 1, 2)
            route_places(B - 2)
            residual(B - 1, 3)
            aggregate(1, B - 1, stats2_ready, ln2_var)
            scale(UNITS - 3)
            ln2_apply(B - 1)
            low(UNITS - 4)
            scale(UNITS - 2)
            route_logits(B - 1)
            route_first(B - 1)
            route_second(B - 1)
            route_gates(B - 1)
            route_places(B - 1)
            low(UNITS - 3)
            low(UNITS - 2)
            scale(UNITS - 1)

            dve.wait_ge(gate_ready, B)

            def per_tile(a):
                return a.unsqueeze(2).to_broadcast([P, TILES, E])

            def per_expert(a):
                return a.unsqueeze(1).to_broadcast([P, TILES, E])

            count, tiles, last, first = (by_expert[:, k, :] for k in range(4))
            ended, mine, less_tile, first_tile, offset, start, region = (by_tile[:, k, :] for k in range(7))
            product, belongs = tile_expert[:, 0], tile_expert[:, 1]
            link(nc.vector.tensor_tensor(count, nextrow[:, B, :], base[:], ALU.subtract))
            link(nc.vector.tensor_tensor(below, count.unsqueeze(2).to_broadcast([P, E, N // TR]),
                                         steps[:].unsqueeze(1).to_broadcast([P, E, N // TR]), ALU.is_gt))
            link(nc.vector.tensor_reduce(tiles, below, AX.X, ALU.add))
            link(nc.vector.tensor_tensor_scan(last, tiles, none[:], 0.0, ALU.add, ALU.add))
            link(nc.vector.tensor_tensor(first, last, tiles, ALU.subtract))
            link(nc.vector.tensor_tensor(product, per_tile(tile_no[:]), per_expert(last), ALU.is_ge))
            link(nc.vector.tensor_reduce(ended, product, AX.X, ALU.add))
            link(nc.vector.tensor_scalar(mine, ended, float(E - 1), None, ALU.min))
            nc.vector.tensor_copy(expert_of[:], mine)
            nc.vector.tensor_scalar(rank_of[:], mine, -1.0, float(E), ALU.mult, ALU.add)
            link(nc.vector.tensor_tensor(belongs, per_tile(mine), per_expert(expert_no[:]), ALU.is_equal))
            link(nc.vector.tensor_tensor(product, belongs, per_expert(count), ALU.mult))
            link(nc.vector.tensor_reduce(less_tile, product, AX.X, ALU.add))
            link(nc.vector.tensor_tensor(product, belongs, per_expert(first), ALU.mult))
            link(nc.vector.tensor_reduce(first_tile, product, AX.X, ALU.add))
            link(nc.vector.tensor_scalar(less_tile, less_tile, float(TR), None, ALU.subtract))
            link(nc.vector.tensor_tensor(offset, tile_no[:], first_tile, ALU.subtract))
            link(nc.vector.tensor_scalar(offset, offset, float(TR), None, ALU.mult))
            link(nc.vector.tensor_tensor(start, offset, less_tile, ALU.min))
            link(nc.vector.tensor_scalar(region, mine, float(REGION), float(TR), ALU.mult, ALU.add))
            nc.vector.tensor_tensor(row_of[:], start, region, ALU.add)
            nc.vector.tensor_tensor(again[:], offset, start, ALU.subtract).then_inc(tables_ready, 1)

            low(UNITS - 1)
            for u in range(0, UNITS, 2):
                nc.vector.tensor_tensor(undo[:, u // 2:u // 2 + 1], down[:, u, 1:2].bitcast(F32),
                                        down[:, u + 1, 0:1].bitcast(F32), ALU.mult)

            dve.wait_ge(tables_ready, 1)

            def take_tile(t):
                dve.wait_ge(turned, t + 1)
                src = xT_ps[:].rearrange("p (c n) -> p c n", c=DC)
                nc.vector.tensor_copy(xh[:], src).then_inc(xs_high, 1)
                dve.wait_ge(xs_high, t + 1)
                nc.vector.tensor_tensor(xl[:], src, xh[:], ALU.subtract).then_inc(xs_ready, 1)

            def split(t, s, e):
                dve.wait_ge(g_ready, t * QUARTERS + (s + 1))
                m = slice(s * MQ, (s + 1) * MQ)
                by = up[:, bass.ds(e * 2, 1), 1:2].rearrange("p a n -> p (a n)").bitcast(F32)
                nc.vector.tensor_scalar(gh[:, m, :], g[:, m, :], by, None, ALU.mult).then_inc(g_high, 1)
                dve.wait_ge(g_high, t * QUARTERS + (s + 1))
                nc.vector.scalar_tensor_tensor(out=gl[:, m, :], in0=g[:, m, :], scalar=by, in1=gh[:, m, :],
                                               op0=ALU.mult, op1=ALU.subtract).then_inc(gs_ready, 1)

            def mark(t, u, slot):
                if not isinstance(t, int) or t >= 2:
                    dve.wait_ge(added, t * 32 - 32)
                first, second, choice, token_no = (xt[:, slot, :, D + k] for k in range(4))
                rank = rank_of[:, bass.ds(t, 1)]
                nc.vector.scalar_tensor_tensor(out=gates[:, 0, :], in0=choice, scalar=rank, in1=first,
                                               op0=ALU.is_equal, op1=ALU.mult).then_inc(marked, 1)
                nc.vector.scalar_tensor_tensor(out=gates[:, 1, :], in0=choice, scalar=rank, in1=second,
                                               op0=ALU.not_equal, op1=ALU.mult).then_inc(marked, 1)
                nc.vector.tensor_scalar(moved[:, 0, :], lane[:], again[:, bass.ds(t, 1)], None,
                                        ALU.is_lt).then_inc(marked, 1)
                nc.vector.tensor_tensor(moved[:, 1, :], spare[:], token_no, ALU.subtract).then_inc(marked, 1)
                dve.wait_ge(marked, t * 6 + 4)
                nc.vector.tensor_tensor(gates[:, 2, :], gates[:, 0, :], gates[:, 1, :], ALU.add).then_inc(marked, 1)
                nc.vector.tensor_tensor(moved[:, 2, :], moved[:, 0, :], moved[:, 1, :], ALU.mult).then_inc(marked, 1)
                dve.wait_ge(marked, t * 6 + 6)
                nc.vector.tensor_tensor(idx[:, u, :], moved[:, 2, :], token_no, ALU.add)

            def result(t, u, r, e):
                dve.wait_ge(y_full, t * 2 + (r + 1))
                nc.vector.scalar_tensor_tensor(out=y1[:, r, :], in0=y_ps[r][:, 0:D], scalar=undo[:, bass.ds(e, 1)],
                                               in1=b2_sb[:, bass.ds(e, 1), :].rearrange("p a n -> p (a n)"),
                                               op0=ALU.mult, op1=ALU.add).then_inc(y_biased, 1)
                dve.wait_ge(y_biased, t * 2 + (r + 1))
                nc.vector.tensor_scalar(y2[:, u, r, :], y1[:, r, :], gates[:, 2, r:r + 1], None,
                                        ALU.mult).then_inc(y_ready, 1)

            def tile(t, u, nxt):
                e = dve.value_load(expert_of[0:1, bass.ds(t, 1)], min_val=0, max_val=E - 1)
                for s in range(QUARTERS):
                    split(t, s, e)
                if nxt:
                    take_tile(t + 1)
                mark(t, u, u)
                for r in range(2):
                    result(t, u, r, e)

            take_tile(0)
            dve.wait_ge(b2_in, 16)
            tile(0, 0, True)
            tile(1, 1, True)
            with dve.Fori(2, TILES - 2, 2) as t:
                for k in range(2):
                    tile(t + k, k, True)
            tile(TILES - 1, 0, False)


def kernel(x, ctx_768, L0_xattn_Wq, L0_xattn_bq, L0_xattn_Wk, L0_xattn_bk, L0_xattn_Wv, L0_xattn_bv,
           L0_ffn_Wr, L0_ffn_W1, L0_ffn_b1, L0_ffn_W2, L0_ffn_b2):
    import numpy as np
    from concourse import bacc
    from concourse.bass_utils import run_bass_kernel_spmd

    def lay(a, *axes):
        a = np.asarray(a)
        return np.ascontiguousarray(a.transpose(*axes) if axes else a)

    arrays = {
        "x": lay(x),
        "ctxT": lay(ctx_768, 0, 2, 1),
        "Wq": lay(L0_xattn_Wq),
        "bq": lay(np.asarray(L0_xattn_bq).reshape(DC, P), 1, 0),
        "Wk": lay(L0_xattn_Wk),
        "bk": lay(np.asarray(L0_xattn_bk).reshape(DC, P), 1, 0),
        "Wv": lay(L0_xattn_Wv),
        "bv": lay(L0_xattn_bv),
        "WrT": lay(L0_ffn_Wr, 1, 0),
        "W1T": lay(L0_ffn_W1, 0, 2, 1),
        "b1": lay(np.asarray(L0_ffn_b1).reshape(E, MC, P), 2, 0, 1),
        "W2T": lay(L0_ffn_W2, 0, 2, 1),
        "b2": lay(L0_ffn_b2),
    }
    nc = bacc.Bacc("TRN2", target_bir_lowering=False, num_devices=1)
    args = [nc.dram_tensor(n, a.shape, mybir.dt.from_np(a.dtype), kind="ExternalInput").ap() for n, a in arrays.items()]
    out = nc.dram_tensor("out", (N + TR, D), F32, kind="ExternalOutput").ap()
    rows = nc.dram_tensor("rows", (E * REGION, ROW), F32).ap()
    build(nc, *args, rows, out)
    r = run_bass_kernel_spmd(nc, [arrays], core_ids=[0])
    return r.results[0]["out"][:N].reshape(B, LQ, D)
```
